# Optimizing a Trainium2 kernel written in Bass

```python
import numpy as np
import jax
import jax.numpy as jnp

def _softmax(x, axis=-1):
    return jax.nn.softmax(x, axis=axis)

def _gelu(x):
    return jax.nn.gelu(x, approximate=True)

def _silu(x):
    return jax.nn.silu(x)

def _sigmoid(x):
    return jax.nn.sigmoid(x)

def _layernorm(x, axis=-1, eps=1e-05):
    m = jnp.mean(x, axis=axis, keepdims=True)
    v = jnp.var(x, axis=axis, keepdims=True)
    return (x - m) / jnp.sqrt(v + eps)

def _scatter_add(tgt, idx, src, axis=0):
    return tgt.at[idx].add(src)

def _segment_sum(src, seg, n):
    return jax.ops.segment_sum(src, seg, n)
kernel_name = 'mk_adj_resnorm_d1_adj_r2_cbbc6d'

def setup_inputs(seed: int=0):
    np.random.seed(seed)
    _w = jnp.asarray

    def _rec_inputs():
        import jax
        import jax.numpy as jnp
        _gk = jax.random.key(seed)
        x = 7.22e-05 + 1 * jax.random.normal(jax.random.fold_in(_gk, 1), (8, 1024, 128), jnp.float32)
        _a = jax.random.bernoulli(jax.random.fold_in(_gk, 2), 0.015625, (8, 1024, 1024))
        _a = jnp.logical_or(_a, jnp.swapaxes(_a, -1, -2))
        _a = jnp.logical_or(_a, jnp.eye(1024, dtype=bool))
        _af = _a.astype(jnp.float32)
        adj = _af
        return (x, adj)
    x, adj = _rec_inputs()

    def _L0_gnn_setup():
        import jax, jax.numpy as jnp
        import numpy as np
        from jax import lax
        DIM = 128
        EPS = 1e-05

        def _bn(h, g, b, m, v):
            scale = g / jnp.sqrt(v + EPS)
            return h * scale[None, :, None] + (b - m * scale)[None, :, None]

        def _conv1d(h, w, pad):
            return lax.conv_general_dilated(h, w, window_strides=(1,), padding=[(pad, pad)], dimension_numbers=('NCH', 'OIH', 'NCH'))
        key = jax.random.key(seed)
        ks = jax.random.split(key, 16)
        bs, n, d = (16, 1024, DIM)
        s = 0.05
        return {'x': jax.random.normal(ks[0], (bs, n, d), jnp.float32), 'mask': jnp.ones((bs, n, n), jnp.float32), 'w_se': jax.random.normal(ks[1], (3, d), jnp.float32) * s, 'b_se': jnp.zeros((3,), jnp.float32), 'conv1_w': jax.random.normal(ks[2], (d, d, 1), jnp.float32) * s, 'bn1_g': jnp.ones((d,), jnp.float32), 'bn1_b': jnp.zeros((d,), jnp.float32), 'bn1_m': jnp.zeros((d,), jnp.float32), 'bn1_v': jnp.ones((d,), jnp.float32), 'conv2_w': jax.random.normal(ks[3], (d, d, 17), jnp.float32) * s, 'bn2_g': jnp.ones((d,), jnp.float32), 'bn2_b': jnp.zeros((d,), jnp.float32), 'bn2_m': jnp.zeros((d,), jnp.float32), 'bn2_v': jnp.ones((d,), jnp.float32), 'w_msg': jax.random.normal(ks[4], (d, d), jnp.float32) * s, 'b_msg': jnp.zeros((d,), jnp.float32), 'w_ih': jax.random.normal(ks[5], (3 * d, 2 * d), jnp.float32) * s, 'b_ih': jnp.zeros((3 * d,), jnp.float32), 'w_hh': jax.random.normal(ks[6], (3 * d, d), jnp.float32) * s, 'b_hh': jnp.zeros((3 * d,), jnp.float32)}
    _L0_gnn_all = _L0_gnn_setup()
    _L0_gnn_in = {k: v for k, v in _L0_gnn_all.items() if k in ('w_se', 'b_se', 'conv1_w', 'bn1_g', 'bn1_b', 'bn1_m', 'bn1_v', 'conv2_w', 'bn2_g', 'bn2_b', 'bn2_m', 'bn2_v', 'w_msg', 'b_msg', 'w_ih', 'b_ih', 'w_hh', 'b_hh')}
    del _L0_gnn_all
    return {'x': x, 'adj': adj, 'L0_gnn_w_se': _L0_gnn_in['w_se'], 'L0_gnn_b_se': _L0_gnn_in['b_se'], 'L0_gnn_conv1_w': _L0_gnn_in['conv1_w'], 'L0_gnn_bn1_g': _L0_gnn_in['bn1_g'], 'L0_gnn_bn1_b': _L0_gnn_in['bn1_b'], 'L0_gnn_bn1_m': _L0_gnn_in['bn1_m'], 'L0_gnn_bn1_v': _L0_gnn_in['bn1_v'], 'L0_gnn_conv2_w': _L0_gnn_in['conv2_w'], 'L0_gnn_bn2_g': _L0_gnn_in['bn2_g'], 'L0_gnn_bn2_b': _L0_gnn_in['bn2_b'], 'L0_gnn_bn2_m': _L0_gnn_in['bn2_m'], 'L0_gnn_bn2_v': _L0_gnn_in['bn2_v'], 'L0_gnn_w_msg': _L0_gnn_in['w_msg'], 'L0_gnn_b_msg': _L0_gnn_in['b_msg'], 'L0_gnn_w_ih': _L0_gnn_in['w_ih'], 'L0_gnn_b_ih': _L0_gnn_in['b_ih'], 'L0_gnn_w_hh': _L0_gnn_in['w_hh'], 'L0_gnn_b_hh': _L0_gnn_in['b_hh']}

def reference(x, adj, L0_gnn_w_se, L0_gnn_b_se, L0_gnn_conv1_w, L0_gnn_bn1_g, L0_gnn_bn1_b, L0_gnn_bn1_m, L0_gnn_bn1_v, L0_gnn_conv2_w, L0_gnn_bn2_g, L0_gnn_bn2_b, L0_gnn_bn2_m, L0_gnn_bn2_v, L0_gnn_w_msg, L0_gnn_b_msg, L0_gnn_w_ih, L0_gnn_b_ih, L0_gnn_w_hh, L0_gnn_b_hh):
    import jax
    import jax.numpy as jnp

    def _L0_gnn_ref(x, mask, w_se, b_se, conv1_w, bn1_g, bn1_b, bn1_m, bn1_v, conv2_w, bn2_g, bn2_b, bn2_m, bn2_v, w_msg, b_msg, w_ih, b_ih, w_hh, b_hh):
        import jax, jax.numpy as jnp
        import numpy as np
        from jax import lax
        DIM = 128
        EPS = 1e-05

        def _bn(h, g, b, m, v):
            scale = g / jnp.sqrt(v + EPS)
            return h * scale[None, :, None] + (b - m * scale)[None, :, None]

        def _conv1d(h, w, pad):
            return lax.conv_general_dilated(h, w, window_strides=(1,), padding=[(pad, pad)], dimension_numbers=('NCH', 'OIH', 'NCH'))
        d = x.shape[-1]
        xc = jnp.transpose(x, (0, 2, 1))
        h = _bn(_conv1d(xc, conv1_w, 0), bn1_g, bn1_b, bn1_m, bn1_v)
        h = jax.nn.relu(h)
        h = _bn(_conv1d(h, conv2_w, 8), bn2_g, bn2_b, bn2_m, bn2_v)
        x_conv = jnp.transpose(jax.nn.relu(h + xc), (0, 2, 1))
        s = x @ w_se.T + b_se
        sq = jnp.sum(s * s, axis=-1)
        dist = sq[:, :, None] + sq[:, None, :] - 2.0 * jnp.einsum('bnd,bmd->bnm', s, s)
        A = jnp.exp(-dist) * mask
        msg = jax.nn.relu(x @ w_msg.T + b_msg)
        x_nmp = jnp.einsum('bnm,bmd->bnd', A, msg)
        x_in = jnp.concatenate([x_conv, x_nmp], axis=-1)
        gi = x_in @ w_ih.T + b_ih
        gh = x @ w_hh.T + b_hh
        gi_r, gi_z, gi_n = (gi[..., :d], gi[..., d:2 * d], gi[..., 2 * d:])
        gh_r, gh_z, gh_n = (gh[..., :d], gh[..., d:2 * d], gh[..., 2 * d:])
        r = jax.nn.sigmoid(gi_r + gh_r)
        z = jax.nn.sigmoid(gi_z + gh_z)
        nn_ = jnp.tanh(gi_n + r * gh_n)
        return (1.0 - z) * nn_ + z * x
    x = _layernorm(x + _L0_gnn_ref(x, adj, L0_gnn_w_se, L0_gnn_b_se, L0_gnn_conv1_w, L0_gnn_bn1_g, L0_gnn_bn1_b, L0_gnn_bn1_m, L0_gnn_bn1_v, L0_gnn_conv2_w, L0_gnn_bn2_g, L0_gnn_bn2_b, L0_gnn_bn2_m, L0_gnn_bn2_v, L0_gnn_w_msg, L0_gnn_b_msg, L0_gnn_w_ih, L0_gnn_b_ih, L0_gnn_w_hh, L0_gnn_b_hh), axis=-1)
    return x

_drawn_inputs = setup_inputs


def setup_inputs(seed=0):
    import zlib

    import numpy as np

    out = dict(_drawn_inputs(seed))
    spreads = {'L0_gnn_b_se': (0.0, 0.8),
     'L0_gnn_bn1_g': (1.0, 0.6),
     'L0_gnn_bn1_b': (0.0, 0.56),
     'L0_gnn_bn1_m': (0.0, 0.496),
     'L0_gnn_bn1_v': (1.0, 0.6),
     'L0_gnn_bn2_g': (1.0, 0.6),
     'L0_gnn_bn2_b': (0.0, 0.8),
     'L0_gnn_bn2_m': (0.0, 0.794),
     'L0_gnn_bn2_v': (1.0, 0.6),
     'L0_gnn_b_msg': (0.0, 0.1),
     'L0_gnn_b_ih': (0.0, 0.312),
     'L0_gnn_b_hh': (0.0, 0.424)}
    factors = {}
    for name, (base, spread) in spreads.items():
        noise = np.random.default_rng([zlib.crc32(name.encode()), seed]).standard_normal(out[name].shape)
        drawn = base * np.exp(spread * noise) if base else spread * noise
        out[name] = jnp.asarray(drawn.astype(out[name].dtype))
    for name, factor in factors.items():
        out[name] = (out[name] * factor).astype(out[name].dtype)
    return out
```

```python
from contextlib import ExitStack

import concourse.bass as bass
from concourse import mybir

F32 = mybir.dt.float32
F32R = mybir.dt.float32r
ALU = mybir.AluOpType
ACT = mybir.ActivationFunctionType
AX = mybir.AxisListType

P = 128
TAPS = 17
PAD = TAPS // 2
EPS = 1e-5
KROWS = 16
ROFF = 32
SOFF = 4
BANK = 512

W_C1 = 0
W_MSG = W_C1 + P
W_SE = W_MSG + P
W_HH = W_SE + SOFF
W_IHC = W_HH + 3 * P
W_IHN = W_IHC + 3 * P
W_C2 = W_IHN + 3 * P
W_ALL = W_C2 + TAPS * P

(G1, B1, M1, V1, G2, B2, M2, V2, BI_R, BI_Z, BI_N, BH_R, BH_Z, BH_N) = range(14)
(SC1, SH1, SC2, SH2, HB_R, HB_Z, HB_N) = range(7)


def build(nc, xT, adjT, w_c1, w_msg, w_se, w_hh, w_ih, w_c2, vec, b_msg, b_se, out):
    B, D, N = xT.shape
    NC = N // P
    HALVES = N // BANK
    PAIR = 2
    SLOTS = NC // PAIR
    CPB = 4

    with ExitStack() as ctx:
        def sb(name, shape, dt=F32):
            return ctx.enter_context(nc.sbuf_tensor(name, shape, dt))

        def pb(name, shape):
            return ctx.enter_context(nc.psum_tensor(name, shape, F32))

        def sem(name):
            return ctx.enter_context(nc.semaphore(name))

        w_hi = sb("w_hi", [P, W_ALL], F32R)
        w_lo = sb("w_lo", [P, W_ALL], F32R)
        vecs = sb("vecs", [P, 14])
        dv = sb("dv", [P, 7])
        bmsg = sb("bmsg", [P, NC, P])
        bse = sb("bse", [P, NC, SOFF])
        ident = sb("ident", [P, P])
        bn_var = sb("bn_var", [P, 2])
        neg_half = sb("neg_half", [P, NC])
        adj_ring = sb("adj_ring", [P, SLOTS, PAIR, N])
        x_f = [sb(f"x_f{p}", [P, N]) for p in range(2)]
        x_hi = [sb(f"x_hi{p}", [P, N], F32R) for p in range(2)]
        x_lo = [sb(f"x_lo{p}", [P, N], F32R) for p in range(2)]
        x_gate = sb("x_gate", [P, N])
        h_f = sb("h_f", [P, N])
        h_hi = [sb(f"h_hi{p}", [P, N + 2 * PAD], F32R) for p in range(2)]
        h_lo = [sb(f"h_lo{p}", [P, N + 2 * PAD], F32R) for p in range(2)]
        msg_f = sb("msg_f", [P, N])
        msg_hi = [sb(f"msg_hi{p}", [P, N], F32R) for p in range(2)]
        msg_lo = [sb(f"msg_lo{p}", [P, N], F32R) for p in range(2)]
        a_f = [sb(f"a_f{k}", [P, N]) for k in range(2)]
        a_hi = [sb(f"a_hi{p}", [P, N], F32R) for p in range(2)]
        a_lo = [sb(f"a_lo{p}", [P, N], F32R) for p in range(2)]
        c_tmp = sb("c_tmp", [P, BANK])
        c_f = sb("c_f", [P, BANK])
        c_hi = sb("c_hi", [P, N], F32R)
        c_lo = sb("c_lo", [P, N], F32R)
        n_hi = sb("n_hi", [P, N], F32R)
        n_lo = sb("n_lo", [P, N], F32R)
        score_l = sb("score_l", [KROWS, N], F32R)
        score_r = sb("score_r", [KROWS, N], F32R)
        s_f = sb("s_f", [P, NC, SOFF])
        s_sq = sb("s_sq", [P, NC, SOFF])
        s_norm = sb("s_norm", [P, NC, 1])
        s_aug = sb("s_aug", [P, NC, P])
        gates = sb("gates", [P, max(3 * N, W_ALL)])
        w_f = gates[:, 0:W_ALL]
        g_r = gates[:, 0:N]
        g_z = gates[:, N:2 * N]
        g_n = gates[:, 2 * N:3 * N]
        stats = sb("stats", [P, NC, 6])
        norm_d = sb("norm_d", [P, NC])
        norm_m = sb("norm_m", [P, NC])
        norm_q = sb("norm_q", [P, NC])
        rstd = sb("rstd", [P, NC])
        y_out = sb("y_out", [P, NC, P])

        ps_s = pb("ps_s", [P, N])
        ps_n = pb("ps_n", [P, N])
        ps_c = pb("ps_c", [P, N])
        ps_m = pb("ps_m", [P, N])

        w_first_in = sem("w_first_in"); w_rest_in = sem("w_rest_in"); v_in = sem("v_in"); x_in = sem("x_in"); xg_in = sem("xg_in")
        adj_in = [sem(f"adj_in{q}") for q in range(SLOTS)]
        y_out_free = sem("y_out_free")
        ident_zero = sem("ident_zero"); ident_set = sem("ident_set")
        w_hi_set = sem("w_hi_set"); w_lo_set = sem("w_lo_set"); se_zero = sem("se_zero")
        consts_set = sem("consts_set"); bn_eps = sem("bn_eps"); bn_rstd = sem("bn_rstd")
        dv_step = sem("dv_step"); dv_set = sem("dv_set"); pads_set = sem("pads_set")
        scores_ready = sem("scores_ready"); nmp_done = sem("nmp_done"); conv2_ready = sem("conv2_ready")
        r_ready = sem("r_ready"); z_ready = sem("z_ready"); hn_ready = sem("hn_ready")
        in_ready = sem("in_ready"); conv1_ready = sem("conv1_ready"); msg_ready = sem("msg_ready")
        s_ready = sem("s_ready"); aug_ready = sem("aug_ready"); yT_ready = sem("yT_ready")
        exp_done = sem("exp_done"); a_hi_set = sem("a_hi_set"); x_hi_set = sem("x_hi_set")
        h_f_set = sem("h_f_set"); h_hi_set = sem("h_hi_set"); msg_hi_set = sem("msg_hi_set")
        c_f_set = sem("c_f_set"); c_hi_set = sem("c_hi_set"); n_hi_set = sem("n_hi_set")
        l_set = sem("l_set"); r_act = sem("r_act"); z_act = sem("z_act"); hn_act = sem("hn_act")
        n_act = sem("n_act")
        masked = sem("masked"); a_lo_set = sem("a_lo_set"); x_lo_set = sem("x_lo_set")
        h_lo_set = sem("h_lo_set"); msg_f_set = sem("msg_f_set"); msg_lo_set = sem("msg_lo_set")
        c_tmp_set = sem("c_tmp_set"); c_lo_set = sem("c_lo_set"); n_lo_set = sem("n_lo_set")
        s_f_set = sem("s_f_set"); s_step = sem("s_step"); aug_set = sem("aug_set")
        r_set = sem("r_set"); rn_set = sem("rn_set"); pre_n_set = sem("pre_n_set")
        y_step = sem("y_step"); y_set = sem("y_set"); stats_set = sem("stats_set")
        norm_step = sem("norm_step"); var_set = sem("var_set"); out_set = sem("out_set")
        rstd_set = sem("rstd_set")

        block = ctx.enter_context(nc.Block())

        def runs(eng, batch):
            batch(0, 0, True, False)
            with eng.Fori(0, (B - 2) // 2) as i:
                batch(i * 2 + 1, 1, False, False)
                batch(i * 2 + 2, 0, False, False)
            batch(B - 1, (B - 1) % 2, False, True)

        @block.sync
        def _(sp):
            def load_x(b, p):
                sp.dma_start(x_f[p][:], xT[b]).then_inc(x_in, 16)

            def load_adj(b, q):
                src = adjT[b, q * PAIR * P:(q + 1) * PAIR * P, :].rearrange("(j p) n -> p j n", p=P)
                sp.dma_start(adj_ring[:, q], src).then_inc(adj_in[q], 16)

            load_x(0, 0)
            sp.dma_start(w_f[:, W_C1:W_C1 + P], w_c1).then_inc(w_first_in, 16)
            sp.dma_start(w_f[:, W_MSG:W_MSG + P], w_msg).then_inc(w_first_in, 16)
            sp.dma_start(w_f[:, W_SE:W_SE + 3], w_se).then_inc(w_first_in, 16)
            sp.dma_start(vecs[:], vec).then_inc(v_in, 16)
            for c in range(NC):
                sp.dma_start(bmsg[:, c, :], b_msg.partition_broadcast(P)).then_inc(v_in, 16)
                sp.dma_start(bse[:, c, 0:3], b_se.partition_broadcast(P)).then_inc(v_in, 16)
            sp.dma_start(w_f[:, W_C2:W_ALL], w_c2).then_inc(w_rest_in, 16)
            load_adj(0, 0)
            sp.dma_start(w_f[:, W_HH:W_HH + 3 * P], w_hh).then_inc(w_rest_in, 16)
            sp.dma_start(w_f[:, W_IHC:W_IHC + 3 * P], w_ih[0:P, :]).then_inc(w_rest_in, 16)
            sp.dma_start(w_f[:, W_IHN:W_IHN + 3 * P], w_ih[P:2 * P, :]).then_inc(w_rest_in, 16)
            for q in range(1, SLOTS):
                load_adj(0, q)

            def load_x_gate(g):
                sp.dma_start(x_gate[:], xT[g]).then_inc(xg_in, 16)

            def store(g):
                sp.wait_ge(out_set, g + 1)
                sp.dma_start(out[g].rearrange("(c p) d -> p c d", p=P), y_out[:]).then_inc(y_out_free, 16)

            def batch(b, p, first, last):
                if not last:
                    if first:
                        sp.wait_ge(x_lo_set, 1)
                    else:
                        sp.wait_ge(c_tmp_set, b * HALVES)
                    load_x(b + 1, 1 - p)
                if not first:
                    load_x_gate(b - 1)
                if not last:
                    for q in range(SLOTS):
                        sp.wait_ge(masked, b * NC + PAIR * (q + 1))
                        load_adj(b + 1, q)
                if not first:
                    store(b - 1)

            runs(sp, batch)
            load_x_gate(B - 1)
            store(B - 1)
            sp.wait_ge(y_out_free, 16 * (B + 1))

        @block.tensor
        def _(pe):
            def three(outs, w0, w1, rhs_hi, rhs_lo, first, last):
                w_h, w_l = w_hi[:, w0:w1], w_lo[:, w0:w1]
                for lhs, rhs, k in ((w_h, rhs_hi, 0), (w_h, rhs_lo, 1), (w_l, rhs_hi, 2)):
                    for o, r in zip(outs, rhs):
                        mm = pe.matmul(o, lhs, r, start=(first and k == 0), stop=(last and k == 2))
                return mm

            def banks(t, off=0):
                return [t[:, off + h * BANK:off + (h + 1) * BANK] for h in range(HALVES)]

            def scores(b, c):
                if c == 0:
                    pe.wait_ge(l_set, b + 1)
                    pe.wait_ge(r_set, b + 1)
                else:
                    pe.wait_ge(masked, b * NC + c)
                for o, r in zip(banks(ps_s), banks(score_r)):
                    mm = pe.matmul(o, score_l[:, c * P:(c + 1) * P], r, start=True, stop=True)
                mm.then_inc(scores_ready, 1)

            def sum_messages(b, p, c, first):
                if c == 0:
                    pe.wait_ge(msg_lo_set, b + 1)
                    if not first:
                        pe.wait_ge(n_lo_set, b)
                pe.wait_ge(a_lo_set, b * NC + c + 1)
                m_h, m_l = (t[p][:, c * P:(c + 1) * P] for t in (msg_hi, msg_lo))
                a_h, a_l = banks(a_hi[c % 2]), banks(a_lo[c % 2])
                for lhs, rhs, k in ((m_h, a_h, 0), (m_h, a_l, 1), (m_l, a_h, 2)):
                    for o, r in zip(banks(ps_n), rhs):
                        mm = pe.matmul(o, lhs, r, start=(c == 0 and k == 0), stop=(c == NC - 1 and k == 2))
                mm.then_inc(nmp_done, 1)

            conv_passes = [(k, s) for k in range(TAPS) for s in range(3)]
            parts = NC // HALVES
            per_part = -(-len(conv_passes) // parts)

            def conv2(b, p, c, first):
                half, part = divmod(c, parts)
                if c == 0:
                    pe.wait_ge(h_lo_set, b + 1)
                if part == 0 and not first:
                    pe.wait_ge(c_tmp_set, (b - 1) * HALVES + half + 1)
                for n in range(part * per_part, min((part + 1) * per_part, len(conv_passes))):
                    k, s = conv_passes[n]
                    w = (w_lo if s == 2 else w_hi)[:, W_C2 + k * P:W_C2 + (k + 1) * P]
                    h = (h_lo if s == 1 else h_hi)[p][:, half * BANK + k:half * BANK + k + BANK]
                    mm = pe.matmul(ps_c[:, half * BANK:(half + 1) * BANK], w, h,
                                   start=(n == 0), stop=(n == len(conv_passes) - 1))
                if part == parts - 1:
                    mm.then_inc(conv2_ready, 1)

            def conv1(n, p):
                pe.wait_ge(x_lo_set, n + 1)
                three(banks(ps_m), W_C1, W_C1 + P, banks(x_hi[p]), banks(x_lo[p]),
                      True, True).then_inc(conv1_ready, 1)

            def by_node(n, p, ps, w0, width):
                for c in range(NC):
                    o = ps[:, c * width:(c + 1) * width]
                    for k, (x, w) in enumerate(((x_hi, w_hi), (x_hi, w_lo), (x_lo, w_hi))):
                        mm = pe.matmul(o, x[p][:, c * P:(c + 1) * P], w[:, w0:w0 + width],
                                       start=(k == 0), stop=(k == 2))
                return mm

            def score_operands(n):
                pe.wait_ge(aug_set, n + 1)
                for c in range(NC):
                    mm = pe.transpose(ps_s[:, c * P:(c + 1) * P], s_aug[:, c, :], ident[:])
                mm.then_inc(aug_ready, 1)

            def gate_hn(g, p):
                three(banks(ps_m), W_HH + 2 * P, W_HH + 3 * P, banks(x_hi[p]), banks(x_lo[p]),
                      True, True).then_inc(hn_ready, 1)

            def gate_rz(g, p, j, ready):
                three(banks(ps_m), W_HH + j * P, W_HH + (j + 1) * P, banks(x_hi[p]), banks(x_lo[p]),
                      True, False)
                three(banks(ps_m), W_IHC + j * P, W_IHC + (j + 1) * P, banks(c_hi), banks(c_lo),
                      False, False)
                three(banks(ps_m), W_IHN + j * P, W_IHN + (j + 1) * P, banks(n_hi), banks(n_lo),
                      False, True).then_inc(ready, 1)

            def gate_r(g, p):
                pe.wait_ge(hn_act, g + 1)
                pe.wait_ge(c_lo_set, (g + 1) * HALVES)
                pe.wait_ge(n_lo_set, g + 1)
                gate_rz(g, p, 0, r_ready)

            def gate_z(g, p):
                pe.wait_ge(r_act, g + 1)
                gate_rz(g, p, 1, z_ready)

            def gate_in(g):
                pe.wait_ge(z_act, g + 1)
                three(banks(ps_m), W_IHC + 2 * P, W_IHC + 3 * P, banks(c_hi), banks(c_lo), True, False)
                three(banks(ps_m), W_IHN + 2 * P, W_IHN + 3 * P, banks(n_hi), banks(n_lo),
                      False, True).then_inc(in_ready, 1)

            def turn_y(g):
                pe.wait_ge(y_set, g + 1)
                for c in range(NC):
                    mm = pe.transpose(ps_m[:, c * P:(c + 1) * P], g_r[:, c * P:(c + 1) * P], ident[:])
                mm.then_inc(yT_ready, 1)

            def batch(b, p, first, last):
                for c in range(NC):
                    if c == NC - 1 and not last:
                        pe.wait_ge(s_f_set, b + 2)
                    scores(b, c)
                    if c == 0 and not first:
                        sum_messages(b - 1, 1 - p, NC - 1, False)
                    if not first:
                        if c == 1:
                            gate_hn(b - 1, 1 - p)
                        if c == 2:
                            gate_r(b - 1, 1 - p)
                        if c == 3:
                            gate_z(b - 1, 1 - p)
                        if c == 4:
                            gate_in(b - 1)
                    if c == 5 and not last:
                        if not first:
                            pe.wait_ge(pre_n_set, b)
                        conv1(b + 1, 1 - p)
                    if c == 6 and not last:
                        pe.wait_ge(h_hi_set, b + 2)
                        by_node(b + 1, 1 - p, ps_m, W_MSG, P).then_inc(msg_ready, 1)
                    if c == 7:
                        if not last:
                            pe.wait_ge(msg_f_set, b + 2)
                        if not first:
                            turn_y(b - 1)
                    conv2(b, p, c, first)
                    if c > 0:
                        sum_messages(b, p, c - 1, first)
                    if c == 6 and not last:
                        pe.wait_ge(masked, b * NC + c + 1)
                        by_node(b + 1, 1 - p, ps_s, W_SE, SOFF).then_inc(s_ready, 1)
                    if c == 7 and not last:
                        pe.wait_ge(masked, (b + 1) * NC)
                        score_operands(b + 1)

            pe.wait_ge(ident_set, 1)
            pe.wait_ge(w_lo_set, 1)
            conv1(0, 0)
            pe.wait_ge(h_hi_set, 1)
            by_node(0, 0, ps_m, W_MSG, P).then_inc(msg_ready, 1)
            by_node(0, 0, ps_s, W_SE, SOFF).then_inc(s_ready, 1)
            score_operands(0)
            pe.wait_ge(w_lo_set, 2)
            pe.wait_ge(pads_set, 4)
            pe.wait_ge(msg_f_set, 1)
            runs(pe, batch)
            p = (B - 1) % 2
            sum_messages(B - 1, p, NC - 1, False)
            pe.wait_ge(out_set, B - 1)
            gate_hn(B - 1, p)
            gate_r(B - 1, p)
            gate_z(B - 1, p)
            gate_in(B - 1)
            turn_y(B - 1)

        @block.scalar
        def _(act):
            def exps(b, c):
                act.wait_ge(scores_ready, b * NC + c + 1)
                act.activation(ps_s[:], ps_s[:], ACT.Exp, scale=-1.0).then_inc(exp_done, 1)

            def a_high(b, c, first):
                if not (first and c < 2):
                    act.wait_ge(nmp_done, b * NC + c - 1)
                act.wait_ge(masked, b * NC + c + 1)
                act.copy(a_hi[c % 2][:], a_f[c % 2][:]).then_inc(a_hi_set, 1)

            def x_high(n, p, reused):
                act.wait_ge(x_in, 16 * (n + 1))
                if reused:
                    act.wait_ge(z_ready, n - 1)
                act.copy(x_hi[p][:], x_f[p][:]).then_inc(x_hi_set, 1)

            def h_high(n, p, reused, prev):
                act.wait_ge(conv1_ready, n + 1)
                if prev:
                    act.wait_ge(h_lo_set, n)
                act.activation(h_f[:], ps_m[:], ACT.Relu, bias=dv[:, SH1:SH1 + 1],
                               scale=dv[:, SC1:SC1 + 1]).then_inc(h_f_set, 1)
                if reused:
                    act.wait_ge(conv2_ready, (n - 1) * HALVES)
                act.activation(h_hi[p][:, PAD:PAD + N], ps_m[:], ACT.Relu, bias=dv[:, SH1:SH1 + 1],
                               scale=dv[:, SC1:SC1 + 1]).then_inc(h_hi_set, 1)

            def msg_high(n, p, reused):
                act.wait_ge(msg_f_set, n + 1)
                if reused:
                    act.wait_ge(nmp_done, (n - 1) * NC)
                act.activation(msg_hi[p][:], msg_f[:], ACT.Relu).then_inc(msg_hi_set, 1)

            def left_operand(n):
                act.wait_ge(aug_ready, n + 1)
                act.copy(score_l[:], ps_s[0:KROWS, :]).then_inc(l_set, 1)

            def c_high(n, half, prev):
                act.wait_ge(c_tmp_set, n * HALVES + half + 1)
                if prev or half:
                    act.wait_ge(c_lo_set, n * HALVES + half)
                act.activation(c_f[:], c_tmp[:], ACT.Relu, bias=dv[:, SH2:SH2 + 1]).then_inc(c_f_set, 1)
                if prev:
                    act.wait_ge(in_ready, n)
                act.activation(c_hi[:, half * BANK:(half + 1) * BANK], c_tmp[:], ACT.Relu,
                               bias=dv[:, SH2:SH2 + 1]).then_inc(c_hi_set, 1)

            def n_high(n, prev):
                act.wait_ge(nmp_done, (n + 1) * NC)
                if prev:
                    act.wait_ge(in_ready, n)
                act.copy(n_hi[:], ps_n[:]).then_inc(n_hi_set, 1)

            def act_hn(g):
                act.wait_ge(hn_ready, g + 1)
                act.activation(g_n, ps_m[:], ACT.Identity, bias=dv[:, HB_N:HB_N + 1],
                               scale=0.5).then_inc(hn_act, 1)

            def act_r(g):
                act.wait_ge(r_ready, g + 1)
                act.activation(g_r, ps_m[:], ACT.Tanh, bias=dv[:, HB_R:HB_R + 1],
                               scale=0.5).then_inc(r_act, 1)

            def act_z(g):
                act.wait_ge(z_ready, g + 1)
                act.activation(g_z, ps_m[:], ACT.Tanh, bias=dv[:, HB_Z:HB_Z + 1],
                               scale=0.5).then_inc(z_act, 1)

            def act_n(g):
                act.wait_ge(pre_n_set, g + 1)
                act.activation(g_r, g_r, ACT.Tanh, bias=vecs[:, BI_N:BI_N + 1]).then_inc(n_act, 1)

            def batch(b, p, first, last):
                for c in range(NC):
                    exps(b, c)
                    a_high(b, c, first)
                    if not first:
                        if c == 0:
                            c_high(b - 1, 1, True)
                            n_high(b - 1, True)
                        if c == 1:
                            act_hn(b - 1)
                        if c == 2:
                            act_r(b - 1)
                        if c == 3:
                            act_z(b - 1)
                    if c == 4 and not last:
                        x_high(b + 1, 1 - p, not first)
                    if c == 4 and not first:
                        act_n(b - 1)
                    if c == 5 and not last:
                        h_high(b + 1, 1 - p, not first, True)
                    if c == 6:
                        if not last:
                            msg_high(b + 1, 1 - p, not first)
                        c_high(b, 0, not first)
                    if c == 7 and not last:
                        left_operand(b + 1)

            x_high(0, 0, False)
            act.wait_ge(dv_set, 1)
            h_high(0, 0, False, False)
            msg_high(0, 0, False)
            left_operand(0)
            runs(act, batch)
            c_high(B - 1, 1, True)
            n_high(B - 1, True)
            act_hn(B - 1)
            act_r(B - 1)
            act_z(B - 1)
            act_n(B - 1)

        @block.vector
        def _(dve):
            def mask(b, c, first):
                if not (first and c < 2):
                    dve.wait_ge(a_lo_set, b * NC + c - 1)
                dve.wait_ge(exp_done, b * NC + c + 1)
                if c % PAIR == 0:
                    dve.wait_ge(adj_in[c // PAIR], 16 * (b + 1))
                dve.tensor_tensor(a_f[c % 2][:], ps_s[:], adj_ring[:, c // PAIR, c % PAIR, :],
                                  ALU.mult).then_inc(masked, 1)

            def a_low(b, c):
                dve.wait_ge(a_hi_set, b * NC + c + 1)
                dve.tensor_tensor(a_lo[c % 2][:], a_f[c % 2][:], a_hi[c % 2][:].bitcast(F32),
                                  ALU.subtract).then_inc(a_lo_set, 1)

            def x_low(n, p):
                dve.wait_ge(x_hi_set, n + 1)
                dve.tensor_tensor(x_lo[p][:], x_f[p][:], x_hi[p][:].bitcast(F32),
                                  ALU.subtract).then_inc(x_lo_set, 1)

            def h_low(n, p):
                dve.wait_ge(h_hi_set, n + 1)
                dve.tensor_tensor(h_lo[p][:, PAD:PAD + N], h_f[:], h_hi[p][:, PAD:PAD + N].bitcast(F32),
                                  ALU.subtract).then_inc(h_lo_set, 1)

            def msg_full(n, prev):
                if prev:
                    dve.wait_ge(msg_lo_set, n)
                dve.wait_ge(msg_ready, n + 1)
                dve.tensor_tensor(msg_f[:], ps_m[:], bmsg[:].rearrange("p c d -> p (c d)"),
                                  ALU.add).then_inc(msg_f_set, 1)

            def msg_low(n, p):
                dve.wait_ge(msg_hi_set, n + 1)
                dve.scalar_tensor_tensor(out=msg_lo[p][:], in0=msg_f[:], scalar=0.0,
                                         in1=msg_hi[p][:].bitcast(F32), op0=ALU.max,
                                         op1=ALU.subtract).then_inc(msg_lo_set, 1)

            STEPS = 10

            def score_rows(n, prev):
                def rows(a, z, right=False):
                    o = ROFF if right else 0
                    return s_aug[:, :, o + a:o + z]

                def done(ins, k):
                    ins.then_inc(s_step, 1)
                    return n * STEPS + k

                if prev:
                    dve.wait_ge(aug_set, n)
                dve.wait_ge(s_ready, n + 1)
                dve.tensor_tensor(s_f[:], ps_s[:, 0:NC * SOFF].rearrange("p (c k) -> p c k", c=NC),
                                  bse[:], ALU.add).then_inc(s_f_set, 1)
                dve.wait_ge(s_f_set, n + 1)
                done(dve.tensor_tensor(s_sq[:], s_f[:], s_f[:], ALU.mult), 1)
                at_hi = done(dve.tensor_copy(rows(0, 3).bitcast(F32R), s_f[:, :, 0:3]), 2)
                dve.wait_ge(s_step, at_hi)
                at_norm = done(dve.tensor_reduce(s_norm[:], s_sq[:, :, 0:3], AX.X, ALU.add), 3)
                at_lo = done(dve.tensor_tensor(rows(3, 6).bitcast(F32R), s_f[:, :, 0:3], rows(0, 3),
                                               ALU.subtract), 4)
                dve.wait_ge(s_step, at_norm)
                at_qhi = done(dve.tensor_copy(rows(12, 13).bitcast(F32R), s_norm[:]), 5)
                dve.wait_ge(s_step, at_lo)
                done(dve.tensor_copy(rows(6, 12), rows(0, 6)), 6)
                dve.wait_ge(s_step, at_qhi)
                at_qlo = done(dve.tensor_tensor(rows(13, 14).bitcast(F32R), s_norm[:], rows(12, 13),
                                                ALU.subtract), 7)
                done(dve.tensor_scalar(rows(0, 6, True), rows(0, 6), -2.0, None, ALU.mult), 8)
                done(dve.tensor_scalar(rows(6, 9, True), rows(3, 6), -2.0, None, ALU.mult), 9)
                done(dve.tensor_scalar(rows(9, 12, True), rows(0, 3), -2.0, None, ALU.mult), 10)
                dve.wait_ge(s_step, at_qlo)
                dve.tensor_copy(rows(14, 16, True), rows(12, 14)).then_inc(aug_set, 1)

            def right_operand(n):
                dve.wait_ge(aug_ready, n + 1)
                dve.tensor_copy(score_r[:], ps_s[ROFF:ROFF + KROWS, :]).then_inc(r_set, 1)

            def c_temp(n, p, half):
                dve.wait_ge(conv2_ready, n * HALVES + half + 1)
                cols = slice(half * BANK, (half + 1) * BANK)
                dve.scalar_tensor_tensor(out=c_tmp[:], in0=ps_c[:, cols], scalar=dv[:, SC2:SC2 + 1],
                                         in1=x_f[p][:, cols], op0=ALU.mult,
                                         op1=ALU.add).then_inc(c_tmp_set, 1)

            def c_low(n, half):
                dve.wait_ge(c_hi_set, n * HALVES + half + 1)
                cols = slice(half * BANK, (half + 1) * BANK)
                dve.tensor_tensor(c_lo[:, cols], c_f[:], c_hi[:, cols].bitcast(F32),
                                  ALU.subtract).then_inc(c_lo_set, 1)

            def n_low(n):
                dve.wait_ge(n_hi_set, n + 1)
                dve.tensor_tensor(n_lo[:], ps_n[:], n_hi[:].bitcast(F32), ALU.subtract).then_inc(n_lo_set, 1)

            def reset_n(g):
                dve.wait_ge(r_act, g + 1)
                dve.scalar_tensor_tensor(out=g_n, in0=g_r, scalar=1.0, in1=g_n, op0=ALU.add,
                                         op1=ALU.mult).then_inc(rn_set, 1)

            def pre_n(g):
                dve.wait_ge(in_ready, g + 1)
                dve.wait_ge(rn_set, g + 1)
                dve.tensor_tensor(g_r, ps_m[:], g_n, ALU.add).then_inc(pre_n_set, 1)

            def blend(g):
                dve.wait_ge(n_act, g + 1)
                dve.wait_ge(xg_in, 16 * (g + 1))
                dve.tensor_tensor(g_n, x_gate[:], g_r, ALU.subtract).then_inc(y_step, 1)
                dve.wait_ge(y_step, 3 * g + 1)
                dve.scalar_tensor_tensor(out=g_z, in0=g_z, scalar=1.0, in1=g_n, op0=ALU.add,
                                         op1=ALU.mult).then_inc(y_step, 1)
                dve.wait_ge(y_step, 3 * g + 2)
                dve.scalar_tensor_tensor(out=g_r, in0=g_z, scalar=0.5, in1=g_r, op0=ALU.mult,
                                         op1=ALU.add).then_inc(y_step, 1)

            def add_x(g):
                dve.wait_ge(y_step, 3 * g + 3)
                dve.tensor_tensor(g_r, g_r, x_gate[:], ALU.add).then_inc(y_set, 1)

            NORM_STEPS = 6

            def norm_stats(g):
                dve.wait_ge(yT_ready, g + 1)
                for c in range(NC):
                    ins = dve.bn_stats(stats[:, c, :], ps_m[:, c * P:(c + 1) * P])
                ins.then_inc(stats_set, 1)
                me, qe, mo, qo = (stats[:, :, k] for k in (1, 2, 4, 5))
                half = P // 2
                dve.wait_ge(stats_set, g + 1)
                dve.tensor_tensor(norm_d[:], me, mo, ALU.subtract).then_inc(norm_step, 1)
                dve.tensor_tensor(norm_m[:], me, mo, ALU.add).then_inc(norm_step, 1)
                dve.tensor_tensor(norm_q[:], qe, qo, ALU.add).then_inc(norm_step, 1)
                dve.wait_ge(norm_step, NORM_STEPS * g + 2)
                dve.tensor_tensor(norm_d[:], norm_d[:], norm_d[:], ALU.mult).then_inc(norm_step, 1)
                dve.tensor_scalar(norm_m[:], norm_m[:], 0.5, None, ALU.mult).then_inc(norm_step, 1)
                dve.wait_ge(norm_step, NORM_STEPS * g + 4)
                dve.scalar_tensor_tensor(out=norm_q[:], in0=norm_d[:], scalar=half / 2, in1=norm_q[:],
                                         op0=ALU.mult, op1=ALU.add).then_inc(norm_step, 1)
                dve.wait_ge(norm_step, NORM_STEPS * g + 6)
                dve.tensor_scalar(rstd[:], norm_q[:], 1.0 / P, EPS, ALU.mult, ALU.add).then_inc(var_set, 1)

            def norm_apply(g):
                dve.wait_ge(rstd_set, g + 1)
                dve.wait_ge(y_out_free, 16 * (g + 1))
                for c in range(NC):
                    ins = dve.tensor_scalar(y_out[:, c, :], ps_m[:, c * P:(c + 1) * P],
                                            norm_m[:, c:c + 1], rstd[:, c:c + 1], ALU.subtract, ALU.mult)
                ins.then_inc(out_set, 1)

            def batch(b, p, first, last):
                for c in range(NC):
                    mask(b, c, first)
                    if c == 0 and not first:
                        c_temp(b - 1, 1 - p, 1)
                    a_low(b, c)
                    if not first:
                        if c == 0:
                            c_low(b - 1, 1)
                            n_low(b - 1)
                        if c == 2:
                            reset_n(b - 1)
                    if c == 4 and not last:
                        x_low(b + 1, 1 - p)
                    if not first:
                        if c == 4:
                            pre_n(b - 1)
                        if c == 5:
                            blend(b - 1)
                            add_x(b - 1)
                    if c == 5 and not last:
                        h_low(b + 1, 1 - p)
                    if c == 6:
                        c_temp(b, p, 0)
                        if not last:
                            msg_full(b + 1, True)
                            msg_low(b + 1, 1 - p)
                        c_low(b, 0)
                        if not last:
                            score_rows(b + 1, True)
                    if c == 7:
                        if not first:
                            norm_stats(b - 1)
                        if not last:
                            right_operand(b + 1)
                        if not first:
                            norm_apply(b - 1)

            for p in range(2):
                for t in (h_hi, h_lo):
                    dve.memset(t[p][:, 0:PAD].bitcast(F32), 0.0)
                    dve.memset(t[p][:, PAD + N:].bitcast(F32), 0.0).then_inc(pads_set, 1)
            dve.memset(s_aug[:], 0.0).then_inc(se_zero, 1)
            dve.wait_ge(se_zero, 1)
            dve.memset(s_aug[:, :, 14:16], 1.0)
            dve.memset(s_aug[:, :, ROFF + 12:ROFF + 14], 1.0)
            dve.memset(bse[:, :, 3:4], 0.0)
            dve.memset(w_f[:, W_SE + 3:W_SE + 4], 0.0).then_inc(se_zero, 1)
            dve.memset(y_out[:, 0, :], 0.0).then_inc(y_out_free, 16)
            x_low(0, 0)

            def split_weights(w0, w1, k):
                dve.tensor_copy(w_hi[:, w0:w1], w_f[:, w0:w1]).then_inc(w_hi_set, 1)
                dve.wait_ge(w_hi_set, k)
                dve.tensor_tensor(w_lo[:, w0:w1], w_f[:, w0:w1], w_hi[:, w0:w1].bitcast(F32),
                                  ALU.subtract).then_inc(w_lo_set, 1)

            dve.wait_ge(se_zero, 2)
            dve.wait_ge(w_first_in, 16 * 3)
            split_weights(W_C1, W_SE + SOFF, 1)
            dve.wait_ge(v_in, 16 * (1 + 2 * NC))
            dve.tensor_scalar(bn_var[:], vecs[:, V1:V2 + 1:V2 - V1], EPS, None, ALU.add).then_inc(bn_eps, 1)
            dve.wait_ge(bn_rstd, 1)
            for k, (g, b, m, sc, sh) in enumerate(((G1, B1, M1, SC1, SH1), (G2, B2, M2, SC2, SH2))):
                dve.tensor_tensor(dv[:, sc:sc + 1], vecs[:, g:g + 1], bn_var[:, k:k + 1],
                                  ALU.mult).then_inc(dv_step, 1)
                dve.wait_ge(dv_step, 2 * k + 1)
                dve.tensor_tensor(bn_var[:, k:k + 1], vecs[:, m:m + 1], dv[:, sc:sc + 1],
                                  ALU.mult).then_inc(dv_step, 1)
                dve.wait_ge(dv_step, 2 * k + 2)
                dve.tensor_tensor(dv[:, sh:sh + 1], vecs[:, b:b + 1], bn_var[:, k:k + 1], ALU.subtract)
            dve.tensor_tensor(dv[:, HB_R:HB_Z + 1], vecs[:, BI_R:BI_Z + 1], vecs[:, BH_R:BH_Z + 1],
                              ALU.add).then_inc(dv_step, 1)
            dve.wait_ge(dv_step, 5)
            dve.tensor_scalar(dv[:, HB_R:HB_Z + 1], dv[:, HB_R:HB_Z + 1], 0.5, None, ALU.mult)
            dve.tensor_scalar(dv[:, HB_N:HB_N + 1], vecs[:, BH_N:BH_N + 1], 0.5, None,
                              ALU.mult).then_inc(dv_set, 1)
            h_low(0, 0)
            msg_full(0, False)
            msg_low(0, 0)
            score_rows(0, False)
            right_operand(0)
            dve.wait_ge(w_rest_in, 16 * 4)
            split_weights(W_HH, W_ALL, 2)
            runs(dve, batch)
            c_temp(B - 1, (B - 1) % 2, 1)
            c_low(B - 1, 1)
            n_low(B - 1)
            reset_n(B - 1)
            pre_n(B - 1)
            blend(B - 1)
            add_x(B - 1)
            norm_stats(B - 1)
            norm_apply(B - 1)

        @block.gpsimd
        def _(pool):
            pool.memset(neg_half[:], -0.5).then_inc(consts_set, 1)
            pool.memset(ident[:], 0.0).then_inc(ident_zero, 1)
            pool.wait_ge(ident_zero, 1)
            pool.affine_select(out=ident[:], in_=ident[:], compare_op=ALU.not_equal, fill=1.0, base=0,
                               pattern=[[-1, P]], channel_multiplier=1).then_inc(ident_set, 1)
            pool.wait_ge(consts_set, 1)
            pool.wait_ge(bn_eps, 1)
            pool.tensor_tensor(bn_var[:], bn_var[:], neg_half[:, 0:2], ALU.pow).then_inc(bn_rstd, 1)

            def norm_scale(g):
                pool.wait_ge(var_set, g + 1)
                pool.tensor_tensor(rstd[:], rstd[:], neg_half[:], ALU.pow).then_inc(rstd_set, 1)

            with pool.Fori(0, B) as g:
                norm_scale(g)


_ORDER = ["xT", "adjT", "w_c1", "w_msg", "w_se", "w_hh", "w_ih", "w_c2", "vec", "b_msg", "b_se"]


def kernel(**inputs):
    import numpy as np
    import concourse.bacc as bacc
    from concourse.bass_utils import run_bass_kernel_spmd

    a = {k.replace("L0_gnn_", ""): np.asarray(v) for k, v in inputs.items()}
    d = a["x"].shape[-1]
    arrays = {
        "xT": a["x"].transpose(0, 2, 1),
        "adjT": a["adj"].transpose(0, 2, 1),
        "w_c1": a["conv1_w"][:, :, 0].T,
        "w_msg": a["w_msg"].T,
        "w_se": a["w_se"].T,
        "w_hh": a["w_hh"].T,
        "w_ih": a["w_ih"].T,
        "w_c2": a["conv2_w"].transpose(1, 2, 0).reshape(d, -1),
        "vec": np.stack([a["bn1_g"], a["bn1_b"], a["bn1_m"], a["bn1_v"],
                         a["bn2_g"], a["bn2_b"], a["bn2_m"], a["bn2_v"],
                         *a["b_ih"].reshape(3, d), *a["b_hh"].reshape(3, d)], axis=1),
        "b_msg": a["b_msg"],
        "b_se": a["b_se"],
    }
    arrays = {k: np.ascontiguousarray(v) for k, v in arrays.items()}
    nc = bacc.Bacc("TRN2", target_bir_lowering=False, num_devices=1)
    args = [nc.dram_tensor(f"{n}_in", arrays[n].shape, F32, kind="ExternalInput").ap() for n in _ORDER]
    out = nc.dram_tensor("out", a["x"].shape, F32, kind="ExternalOutput").ap()
    build(nc, *args, out)
    r = run_bass_kernel_spmd(nc, [{f"{n}_in": arrays[n] for n in _ORDER}], core_ids=[0])
    return r.results[0]["out"]
```

```python
from contextlib import ExitStack

import concourse.bass as bass
from concourse import mybir

F32 = mybir.dt.float32
F32R = mybir.dt.float32r
ALU = mybir.AluOpType
ACT = mybir.ActivationFunctionType
AX = mybir.AxisListType

P = 128
TAPS = 17
PAD = TAPS // 2
GROUPS = -(-TAPS // 3)
FULL = TAPS // 3
EPS = 1e-5
KROWS = 16
ROFF = 32
SOFF = 4
BANK = 512

W_C1 = 0
W_MSG = W_C1 + P
W_SE = W_MSG + P
W_HH = W_SE + SOFF
W_IHC = W_HH + 3 * P
W_IHN = W_IHC + 3 * P
W_C2 = W_IHN + 3 * P
W_RAW = W_C2 + TAPS * P
W_U = [W_C2 + k * GROUPS * P for k in range(4)]
W_ALL = W_U[3] + FULL * P

(G1, B1, M1, V1, G2, B2, M2, V2, BI_R, BI_Z, BI_N, BH_R, BH_Z, BH_N) = range(14)
(SC1, SH1, SC2, SH2, HB_R, HB_Z, HB_N) = range(7)


def build(nc, xT, adjT, w_c1, w_msg, w_se, w_hh, w_ih, w_c2, vec, b_msg, b_se, out):
    B, D, N = xT.shape
    NC = N // P
    HALVES = N // BANK
    SLOTS = 4
    LPB = NC // SLOTS
    T = N // 2
    DW = (N + 2 * PAD - 2) // 2

    with ExitStack() as ctx:
        def sb(name, shape, dt=F32):
            return ctx.enter_context(nc.sbuf_tensor(name, shape, dt))

        def pb(name, shape):
            return ctx.enter_context(nc.psum_tensor(name, shape, F32))

        def sem(name):
            return ctx.enter_context(nc.semaphore(name))

        w_hi = sb("w_hi", [P, W_ALL], F32R)
        w_lo = sb("w_lo", [P, W_ALL], F32R)
        vecs = sb("vecs", [P, 14])
        dv = sb("dv", [P, 7])
        bmsg = sb("bmsg", [P, P])
        bse = sb("bse", [P, NC, SOFF])
        ident = sb("ident", [P, P])
        bn_var = sb("bn_var", [P, 2])
        neg_half = sb("neg_half", [P, NC])
        adj_ring = sb("adj_ring", [P, SLOTS, N])
        x_f = [sb(f"x_f{p}", [P, N]) for p in range(2)]
        x_hi = [sb(f"x_hi{p}", [P, N], F32R) for p in range(2)]
        x_lo = [sb(f"x_lo{p}", [P, N], F32R) for p in range(2)]
        x_gate = sb("x_gate", [P, N])
        h_f = sb("h_f", [P, N + 2 * PAD])
        d_f = sb("d_f", [P, 2, DW])
        d_hi = [sb(f"d_hi{k}", [P, 2, DW], F32R) for k in range(3)]
        d_lo = [sb(f"d_lo{k}", [P, 2, DW], F32R) for k in range(3)]
        msg_hi = [sb(f"msg_hi{p}", [P, N], F32R) for p in range(2)]
        msg_lo = [sb(f"msg_lo{p}", [P, N], F32R) for p in range(2)]
        a_f = [sb(f"a_f{k}", [P, N]) for k in range(2)]
        a_hi = [sb(f"a_hi{p}", [P, N], F32R) for p in range(2)]
        a_lo = [sb(f"a_lo{p}", [P, N], F32R) for p in range(2)]
        m2_f = sb("m2_f", [P, T])
        ab = sb("ab", [P, 2, T])
        c_f = sb("c_f", [P, T])
        c_hi = sb("c_hi", [P, N], F32R)
        c_lo = sb("c_lo", [P, N], F32R)
        n_hi = sb("n_hi", [P, N], F32R)
        n_lo = sb("n_lo", [P, N], F32R)
        score_l = sb("score_l", [KROWS, N], F32R)
        score_r = sb("score_r", [KROWS, N], F32R)
        s_f = sb("s_f", [P, NC, SOFF])
        s_sq = sb("s_sq", [P, NC, SOFF])
        s_norm = sb("s_norm", [P, NC, 1])
        s_aug = sb("s_aug", [P, NC, P])
        gates = sb("gates", [P, N + max(2 * N, W_RAW)])
        w_f = gates[:, N:N + W_RAW]
        g_r = gates[:, 0:N]
        g_z = gates[:, N:2 * N]
        g_n = gates[:, 2 * N:3 * N]
        msg_f = g_r
        y_out = g_z.rearrange("p (c d) -> p c d", c=NC)
        u_f = adj_ring[:, 2:4, :].rearrange("p s n -> p (s n)")[:, 0:2 * GROUPS * P]
        stats = sb("stats", [P, NC, 6])
        norm_d = sb("norm_d", [P, NC])
        norm_m = sb("norm_m", [P, NC])
        norm_q = sb("norm_q", [P, NC])
        rstd = sb("rstd", [P, NC])

        ps_s = pb("ps_s", [P, N])
        ps_n = pb("ps_n", [P, N])
        ps_c = pb("ps_c", [P, N])
        ps_m = pb("ps_m", [P, N])

        CPB = BANK // (P + SOFF)

        def by_node_out(c, a, z):
            ps, c = (ps_m, c) if c < 2 * CPB else (ps_s, c - 2 * CPB)
            at = c // CPB * BANK + c % CPB * (P + SOFF)
            return ps[:, at + a:at + z]

        def by_node_in_m(a, z):
            banks = ps_m[:].rearrange("p (h n) -> p h n", h=2)[:, :, 0:CPB * (P + SOFF)]
            return banks.rearrange("p h (c n) -> p h c n", c=CPB)[:, :, :, a:z]

        def by_node_in_s(a, z):
            rest = ps_s[:, 0:(NC - 2 * CPB) * (P + SOFF)]
            return rest.rearrange("p (c n) -> p c n", n=P + SOFF)[:, :, a:z]

        w_first_in = sem("w_first_in"); w_rest_in = sem("w_rest_in"); v_in = sem("v_in"); x_in = sem("x_in"); xg_in = sem("xg_in")
        adj_in = [sem(f"adj_in{q}") for q in range(SLOTS)]
        y_out_free = sem("y_out_free")
        ident_zero = sem("ident_zero"); ident_set = sem("ident_set")
        w_hi_set = sem("w_hi_set"); w_lo_set = sem("w_lo_set"); w_step = sem("w_step"); se_zero = sem("se_zero")
        consts_set = sem("consts_set"); bn_eps = sem("bn_eps"); bn_rstd = sem("bn_rstd")
        dv_step = sem("dv_step"); dv_set = sem("dv_set"); pads_set = sem("pads_set")
        scores_ready = sem("scores_ready"); nmp_done = sem("nmp_done"); m12_ready = sem("m12_ready")
        m0_ready = sem("m0_ready"); m3_ready = sem("m3_ready")
        r_ready = sem("r_ready"); z_ready = sem("z_ready"); hn_ready = sem("hn_ready")
        in_ready = sem("in_ready"); conv1_ready = sem("conv1_ready"); by_node_ready = sem("by_node_ready")
        aug_ready = sem("aug_ready"); yT_ready = sem("yT_ready")
        d_hi_set = [sem(f"d_hi_set{k}") for k in range(3)]
        exp_done = sem("exp_done"); a_hi_set = sem("a_hi_set"); x_hi_set = sem("x_hi_set")
        h_f_set = sem("h_f_set"); m2_set = sem("m2_set"); msg_hi_set = sem("msg_hi_set")
        c_f_set = sem("c_f_set"); c_hi_set = sem("c_hi_set"); n_hi_set = sem("n_hi_set")
        operands_set = sem("operands_set"); r_act = sem("r_act"); z_act = sem("z_act"); hn_act = sem("hn_act")
        n_act = sem("n_act")
        masked = sem("masked"); a_lo_set = sem("a_lo_set"); m1_used = sem("m1_used")
        ab_set = sem("ab_set"); d_f_set = [sem(f"d_f_set{k}") for k in range(3)]; msg_f_set = sem("msg_f_set"); msg_lo_set = sem("msg_lo_set")
        c_sum_set = [sem("c_even_set"), sem("c_odd_set")]; c_odd_lo_set = sem("c_odd_lo_set"); n_lo_set = sem("n_lo_set")
        s_f_set = sem("s_f_set"); ps_s_left = sem("ps_s_left"); s_step = sem("s_step"); aug_set = sem("aug_set")
        rn_set = sem("rn_set"); pre_n_set = sem("pre_n_set")
        p_set = sem("p_set"); q_set = sem("q_set"); y_set = sem("y_set"); stats_set = sem("stats_set")
        norm_step = sem("norm_step"); var_set = sem("var_set"); normed = sem("normed")
        x_lo_set = sem("x_lo_set"); d_lo_set = [sem(f"d_lo_set{k}") for k in range(3)]
        c_even_lo_set = sem("c_even_lo_set")
        rstd_set = sem("rstd_set")

        block = ctx.enter_context(nc.Block())

        def runs(eng, batch):
            batch(0, 0, True, False)
            with eng.Fori(0, (B - 2) // 2) as i:
                batch(i * 2 + 1, 1, False, False)
                batch(i * 2 + 2, 0, False, False)
            batch(B - 1, (B - 1) % 2, False, True)

        @block.sync
        def _(sp):
            def load_x(b, p):
                sp.dma_start(x_f[p][:], xT[b]).then_inc(x_in, 16)

            def load_adj(b, c):
                sp.dma_start(adj_ring[:, c % SLOTS, :],
                             adjT[b, c * P:(c + 1) * P, :]).then_inc(adj_in[c % SLOTS], 16)

            load_x(0, 0)
            sp.dma_start(w_f[:, W_C1:W_C1 + P], w_c1).then_inc(w_first_in, 16)
            sp.dma_start(w_f[:, W_MSG:W_MSG + P], w_msg).then_inc(w_first_in, 16)
            sp.dma_start(w_f[:, W_SE:W_SE + 3], w_se).then_inc(w_first_in, 16)
            sp.dma_start(vecs[:], vec).then_inc(v_in, 16)
            sp.dma_start(bmsg[:], b_msg.partition_broadcast(P)).then_inc(v_in, 16)
            for c in range(NC):
                sp.dma_start(bse[:, c, 0:3], b_se.partition_broadcast(P)).then_inc(v_in, 16)
            sp.dma_start(w_f[:, W_C2:W_RAW], w_c2).then_inc(w_rest_in, 16)
            load_adj(0, 0)
            sp.dma_start(w_f[:, W_HH:W_HH + 3 * P], w_hh).then_inc(w_rest_in, 16)
            sp.dma_start(w_f[:, W_IHC:W_IHC + 3 * P], w_ih[0:P, :]).then_inc(w_rest_in, 16)
            sp.dma_start(w_f[:, W_IHN:W_IHN + 3 * P], w_ih[P:2 * P, :]).then_inc(w_rest_in, 16)
            load_adj(0, 1)
            sp.wait_ge(w_lo_set, 3)
            load_adj(0, 2)
            load_adj(0, 3)

            def load_x_gate(g):
                sp.dma_start(x_gate[:], xT[g]).then_inc(xg_in, 16)

            def store(g):
                sp.wait_ge(normed, g + 2)
                sp.dma_start(out[g].rearrange("(c p) d -> p c d", p=P), y_out).then_inc(y_out_free, 16)

            def batch(b, p, first, last):
                if not last:
                    if first:
                        sp.wait_ge(x_lo_set, 1)
                    else:
                        sp.wait_ge(ab_set, b)
                    load_x(b + 1, 1 - p)
                if not first:
                    load_x_gate(b - 1)
                for c in range(SLOTS if last else NC):
                    sp.wait_ge(masked, b * NC + c + 1)
                    if c < SLOTS:
                        load_adj(b, c + SLOTS)
                    else:
                        load_adj(b + 1, c - SLOTS)
                if not first:
                    store(b - 1)

            runs(sp, batch)
            load_x_gate(B - 1)
            store(B - 1)
            sp.wait_ge(y_out_free, 16 * (B + 1))

        @block.tensor
        def _(pe):
            def three(outs, w0, w1, rhs_hi, rhs_lo, first, last):
                w_h, w_l = w_hi[:, w0:w1], w_lo[:, w0:w1]
                for lhs, rhs, k in ((w_h, rhs_hi, 0), (w_h, rhs_lo, 1), (w_l, rhs_hi, 2)):
                    for o, r in zip(outs, rhs):
                        mm = pe.matmul(o, lhs, r, start=(first and k == 0), stop=(last and k == 2))
                return mm

            def banks(t, off=0):
                return [t[:, off + h * BANK:off + (h + 1) * BANK] for h in range(HALVES)]

            def scores(b, c):
                if c == 0:
                    pe.wait_ge(operands_set, 2 * (b + 1))
                else:
                    pe.wait_ge(exp_done, b * NC + c)
                for o, r in zip(banks(ps_s), banks(score_r)):
                    mm = pe.matmul(o, score_l[:, c * P:(c + 1) * P], r, start=True, stop=True)
                mm.then_inc(scores_ready, 1)

            def sum_messages(b, p, c, first):
                if c == 0:
                    pe.wait_ge(msg_lo_set, b + 1)
                    if not first:
                        pe.wait_ge(n_lo_set, b)
                pe.wait_ge(a_lo_set, b * NC + c + 1)
                m_h, m_l = (t[p][:, c * P:(c + 1) * P] for t in (msg_hi, msg_lo))
                a_h, a_l = banks(a_hi[c % 2]), banks(a_lo[c % 2])
                for lhs, rhs, k in ((m_h, a_h, 0), (m_h, a_l, 1), (m_l, a_h, 2)):
                    for o, r in zip(banks(ps_n), rhs):
                        mm = pe.matmul(o, lhs, r, start=(c == 0 and k == 0), stop=(c == NC - 1 and k == 2))
                mm.then_inc(nmp_done, 1)

            M1, M2, M0, M3 = (1, 1, 0, GROUPS), (2, 2, 0, GROUPS), (0, 0, 0, GROUPS), (3, 0, 1, FULL)
            conv_passes = [(m, d, at + 3 * g, g, s, g == 0 and s == 0, g == n - 1 and s == 2)
                           for m, d, at, n in (M1, M2, M0, M3) for g in range(n) for s in range(3)]
            conv_until = (12, 14, 16, 22, 36, 42, 55, len(conv_passes))
            bank_of = {1: 0, 2: 1, 0: 0, 3: 1}

            def conv2(b, c, first):
                for n in range(conv_until[c - 1] if c else 0, conv_until[c]):
                    m, d, i, g, s, begins, ends = conv_passes[n]
                    if begins and m != 3:
                        pe.wait_ge(d_lo_set[d], b + 1)
                    if begins and m == 1 and not first:
                        pe.wait_ge(c_sum_set[0], b)
                    if begins and m == 2 and not first:
                        pe.wait_ge(c_sum_set[1], b)
                    if begins and m == 0:
                        pe.wait_ge(m1_used, b + 1)
                    w = (w_lo if s == 2 else w_hi)[:, W_U[m] + g * P:W_U[m] + (g + 1) * P]
                    h = (d_lo if s == 1 else d_hi)[d][:, i % 2, i // 2:i // 2 + T]
                    mm = pe.matmul(ps_c[:, bank_of[m] * T:(bank_of[m] + 1) * T], w, h, start=begins, stop=ends)
                    if ends and m != 1:
                        mm.then_inc({2: m12_ready, 0: m0_ready, 3: m3_ready}[m], 1)

            def conv1(n, p):
                pe.wait_ge(x_lo_set, n + 1)
                three(banks(ps_m), W_C1, W_C1 + P, banks(x_hi[p]), banks(x_lo[p]),
                      True, True).then_inc(conv1_ready, 1)

            def by_node(n, p, left_s):
                for c in range(NC):
                    if c == 2 * CPB and left_s is not None:
                        pe.wait_ge(exp_done, left_s)
                    o = by_node_out(c, 0, P + SOFF)
                    for k, (x, w) in enumerate(((x_hi, w_hi), (x_hi, w_lo), (x_lo, w_hi))):
                        mm = pe.matmul(o, x[p][:, c * P:(c + 1) * P], w[:, W_MSG:W_MSG + P + SOFF],
                                       start=(k == 0), stop=(k == 2))
                mm.then_inc(by_node_ready, 1)

            def score_operands(n):
                pe.wait_ge(aug_set, n + 1)
                for c in range(NC):
                    mm = pe.transpose(ps_s[:, c * P:(c + 1) * P], s_aug[:, c, :], ident[:])
                mm.then_inc(aug_ready, 1)

            def gate_hn(g, p):
                pe.wait_ge(normed, g + 1)
                three(banks(ps_m), W_HH + 2 * P, W_HH + 3 * P, banks(x_hi[p]), banks(x_lo[p]),
                      True, True).then_inc(hn_ready, 1)

            def gate_rz(g, p, j, ready):
                three(banks(ps_m), W_HH + j * P, W_HH + (j + 1) * P, banks(x_hi[p]), banks(x_lo[p]),
                      True, False)
                if j == 0:
                    pe.wait_ge(n_lo_set, g + 1)
                three(banks(ps_m), W_IHN + j * P, W_IHN + (j + 1) * P, banks(n_hi), banks(n_lo),
                      False, False)
                if j == 0:
                    pe.wait_ge(c_even_lo_set, g + 1)
                    pe.wait_ge(c_odd_lo_set, g + 1)
                three(banks(ps_m), W_IHC + j * P, W_IHC + (j + 1) * P, banks(c_hi), banks(c_lo),
                      False, True).then_inc(ready, 1)

            def gate_r(g, p):
                pe.wait_ge(hn_act, g + 1)
                gate_rz(g, p, 0, r_ready)

            def gate_z(g, p):
                pe.wait_ge(r_act, g + 1)
                gate_rz(g, p, 1, z_ready)

            def gate_in(g):
                pe.wait_ge(z_act, g + 1)
                three(banks(ps_m), W_IHC + 2 * P, W_IHC + 3 * P, banks(c_hi), banks(c_lo), True, False)
                three(banks(ps_m), W_IHN + 2 * P, W_IHN + 3 * P, banks(n_hi), banks(n_lo),
                      False, True).then_inc(in_ready, 1)

            def turn_y(g):
                pe.wait_ge(y_set, g + 1)
                for c in range(NC):
                    mm = pe.transpose(ps_m[:, c * P:(c + 1) * P], g_n[:, c * P:(c + 1) * P], ident[:])
                mm.then_inc(yT_ready, 1)

            def batch(b, p, first, last):
                for c in range(NC):
                    if c == 0 and not first:
                        sum_messages(b - 1, 1 - p, NC - 1, False)
                    if c == 6 and not last:
                        pe.wait_ge(ps_s_left, b + 2)
                    scores(b, c)
                    if c == 0 and not first:
                        gate_hn(b - 1, 1 - p)
                    if c < 2:
                        conv2(b, c, first)
                    if not first:
                        if c == 1:
                            gate_r(b - 1, 1 - p)
                        if c == 2:
                            gate_z(b - 1, 1 - p)
                        if c == 3:
                            gate_in(b - 1)
                    if c == 4 and not last:
                        if not first:
                            pe.wait_ge(pre_n_set, b)
                        conv1(b + 1, 1 - p)
                    if c == 5 and not last:
                        pe.wait_ge(h_f_set, b + 2)
                        by_node(b + 1, 1 - p, b * NC + c + 1)
                    if c == 6 and not first:
                        if not last:
                            pe.wait_ge(msg_f_set, b + 2)
                        turn_y(b - 1)
                    if c >= 2:
                        conv2(b, c, first)
                    if c > 0:
                        sum_messages(b, p, c - 1, first)
                    if c == 7 and not last:
                        pe.wait_ge(exp_done, (b + 1) * NC)
                        score_operands(b + 1)

            pe.wait_ge(ident_set, 1)
            pe.wait_ge(w_lo_set, 1)
            conv1(0, 0)
            pe.wait_ge(h_f_set, 1)
            by_node(0, 0, None)
            score_operands(0)
            pe.wait_ge(w_lo_set, 3)
            pe.wait_ge(msg_f_set, 1)
            runs(pe, batch)
            p = (B - 1) % 2
            gate_hn(B - 1, p)
            sum_messages(B - 1, p, NC - 1, False)
            gate_r(B - 1, p)
            gate_z(B - 1, p)
            gate_in(B - 1)
            turn_y(B - 1)

        @block.scalar
        def _(act):
            def exps(b, c, first):
                if not (first and c < 2):
                    act.wait_ge(a_lo_set, b * NC + c - 1)
                act.wait_ge(scores_ready, b * NC + c + 1)
                act.activation(a_f[c % 2][:], ps_s[:], ACT.Exp, scale=-1.0).then_inc(exp_done, 1)

            def a_high(b, c, first):
                if not (first and c < 2):
                    act.wait_ge(nmp_done, b * NC + c - 1)
                act.wait_ge(masked, b * NC + c + 1)
                act.copy(a_hi[c % 2][:], a_f[c % 2][:]).then_inc(a_hi_set, 1)

            def x_high(n, p, reused):
                act.wait_ge(x_in, 16 * (n + 1))
                if reused:
                    act.wait_ge(z_ready, n - 1)
                act.copy(x_hi[p][:], x_f[p][:]).then_inc(x_hi_set, 1)

            def h_full(n, prev):
                act.wait_ge(conv1_ready, n + 1)
                if prev:
                    act.wait_ge(d_lo_set[0], n)
                act.activation(h_f[:, PAD:PAD + N], ps_m[:], ACT.Relu, bias=dv[:, SH1:SH1 + 1],
                               scale=dv[:, SC1:SC1 + 1]).then_inc(h_f_set, 1)

            def d_high(n, d, prev):
                act.wait_ge(d_f_set[d], n + 1)
                if prev:
                    act.wait_ge((m3_ready, m12_ready, m12_ready)[d], n)
                act.copy(d_hi[d][:], d_f[:]).then_inc(d_hi_set[d], 1)

            def copy_m2(n):
                act.wait_ge(m12_ready, n + 1)
                act.copy(m2_f[:], ps_c[:, T:2 * T]).then_inc(m2_set, 1)

            def msg_high(n, p, reused):
                act.wait_ge(msg_f_set, n + 1)
                if reused:
                    act.wait_ge(nmp_done, (n - 1) * NC)
                act.activation(msg_hi[p][:], msg_f, ACT.Relu).then_inc(msg_hi_set, 1)

            def both_operands(n):
                act.wait_ge(aug_ready, n + 1)
                act.copy(score_l[:], ps_s[0:KROWS, :]).then_inc(operands_set, 1)
                act.copy(score_r[:], ps_s[ROFF:ROFF + KROWS, :]).then_inc(operands_set, 1)

            def c_high(n, odd, prev):
                act.wait_ge(c_sum_set[odd], n + 1)
                if odd:
                    act.wait_ge(c_even_lo_set, n + 1)
                elif prev:
                    act.wait_ge(c_odd_lo_set, n)
                    act.wait_ge(in_ready, n)
                act.activation(c_f[:], ab[:, odd, :], ACT.Relu, bias=dv[:, SH2:SH2 + 1]).then_inc(c_f_set, 1)
                act.activation(c_hi[:, odd::2], ab[:, odd, :], ACT.Relu,
                               bias=dv[:, SH2:SH2 + 1]).then_inc(c_hi_set, 1)

            def n_high(n, prev):
                act.wait_ge(nmp_done, (n + 1) * NC)
                if prev:
                    act.wait_ge(in_ready, n)
                act.copy(n_hi[:], ps_n[:]).then_inc(n_hi_set, 1)

            def act_hn(g):
                act.wait_ge(hn_ready, g + 1)
                act.activation(g_n, ps_m[:], ACT.Identity, bias=dv[:, HB_N:HB_N + 1],
                               scale=0.5).then_inc(hn_act, 1)

            def act_r(g):
                act.wait_ge(r_ready, g + 1)
                act.activation(g_r, ps_m[:], ACT.Tanh, bias=dv[:, HB_R:HB_R + 1],
                               scale=0.5).then_inc(r_act, 1)

            def act_z(g):
                act.wait_ge(z_ready, g + 1)
                act.wait_ge(y_out_free, 16 * (g + 1))
                act.activation(g_z, ps_m[:], ACT.Tanh, bias=dv[:, HB_Z:HB_Z + 1],
                               scale=0.5).then_inc(z_act, 1)

            def act_n(g):
                act.wait_ge(pre_n_set, g + 1)
                act.activation(g_r, g_r, ACT.Tanh, bias=vecs[:, BI_N:BI_N + 1]).then_inc(n_act, 1)

            def batch(b, p, first, last):
                for c in range(NC):
                    exps(b, c, first)
                    if c == 0 and not first:
                        n_high(b - 1, True)
                    if c == 3:
                        d_high(b, 0, not first)
                    if c == 4 and not first:
                        act_n(b - 1)
                    if c == 6 and not last:
                        msg_high(b + 1, 1 - p, not first)
                    if c == 7:
                        c_high(b, 0, not first)
                    a_high(b, c, first)
                    if c == 0:
                        if not first:
                            c_high(b - 1, 1, True)
                            act_hn(b - 1)
                        d_high(b, 2, not first)
                    if c == 1 and not first:
                        act_r(b - 1)
                    if c == 2 and not first:
                        act_z(b - 1)
                    if c == 3 and not last:
                        x_high(b + 1, 1 - p, not first)
                    if c == 4:
                        if not last:
                            h_full(b + 1, True)
                        copy_m2(b)
                    if c == 5 and not last:
                        d_high(b + 1, 1, True)
                    if c == 7 and not last:
                        both_operands(b + 1)

            x_high(0, 0, False)
            act.wait_ge(dv_set, 1)
            h_full(0, False)
            d_high(0, 1, False)
            msg_high(0, 0, False)
            both_operands(0)
            runs(act, batch)
            act_hn(B - 1)
            n_high(B - 1, True)
            c_high(B - 1, 1, True)
            act_r(B - 1)
            act_z(B - 1)
            act_n(B - 1)

        @block.vector
        def _(dve):
            def mask(b, c):
                dve.wait_ge(exp_done, b * NC + c + 1)
                dve.wait_ge(adj_in[c % SLOTS], 16 * (b * LPB + c // SLOTS + 1))
                dve.tensor_tensor(a_f[c % 2][:], a_f[c % 2][:], adj_ring[:, c % SLOTS, :],
                                  ALU.mult).then_inc(masked, 1)

            def a_low(b, c):
                dve.wait_ge(a_hi_set, b * NC + c + 1)
                dve.tensor_tensor(a_lo[c % 2][:], a_f[c % 2][:], a_hi[c % 2][:].bitcast(F32),
                                  ALU.subtract).then_inc(a_lo_set, 1)

            def messages_and_s(n, prev):
                if prev:
                    dve.wait_ge(aug_set, n)
                dve.wait_ge(by_node_ready, n + 1)
                m = 2 * CPB
                msg = msg_f.rearrange("p (c d) -> p c d", c=NC)
                dve.tensor_tensor(msg[:, m:, :], by_node_in_s(0, P),
                                  bmsg[:].unsqueeze(1).to_broadcast([P, NC - m, P]), ALU.add)
                dve.tensor_tensor(s_f[:, m:, :], by_node_in_s(P, P + SOFF), bse[:, m:, :],
                                  ALU.add).then_inc(ps_s_left, 1)
                dve.tensor_tensor(s_f[:, 0:m, :].rearrange("p (h c) k -> p h c k", h=2),
                                  by_node_in_m(P, P + SOFF),
                                  bse[:, 0:m, :].rearrange("p (h c) k -> p h c k", h=2),
                                  ALU.add).then_inc(s_f_set, 1)
                dve.tensor_tensor(msg[:, 0:m, :].rearrange("p (h c) d -> p h c d", h=2), by_node_in_m(0, P),
                                  bmsg[:].unsqueeze(1).unsqueeze(1).to_broadcast([P, 2, CPB, P]),
                                  ALU.add).then_inc(msg_f_set, 1)

            def msg_low(n, p):
                dve.wait_ge(msg_hi_set, n + 1)
                dve.scalar_tensor_tensor(out=msg_lo[p][:], in0=msg_f, scalar=0.0,
                                         in1=msg_hi[p][:].bitcast(F32), op0=ALU.max,
                                         op1=ALU.subtract).then_inc(msg_lo_set, 1)

            STEPS = 10

            def score_rows(n):
                def rows(a, z, right=False):
                    o = ROFF if right else 0
                    return s_aug[:, :, o + a:o + z]

                def done(ins, k):
                    ins.then_inc(s_step, 1)
                    return n * STEPS + k

                dve.wait_ge(s_f_set, n + 1)
                done(dve.tensor_tensor(s_sq[:], s_f[:], s_f[:], ALU.mult), 1)
                at_hi = done(dve.tensor_copy(rows(0, 3).bitcast(F32R), s_f[:, :, 0:3]), 2)
                dve.wait_ge(s_step, at_hi)
                at_norm = done(dve.tensor_reduce(s_norm[:], s_sq[:, :, 0:3], AX.X, ALU.add), 3)
                at_lo = done(dve.tensor_tensor(rows(3, 6).bitcast(F32R), s_f[:, :, 0:3], rows(0, 3),
                                               ALU.subtract), 4)
                dve.wait_ge(s_step, at_norm)
                at_qhi = done(dve.tensor_copy(rows(12, 13).bitcast(F32R), s_norm[:]), 5)
                dve.wait_ge(s_step, at_lo)
                done(dve.tensor_copy(rows(6, 12), rows(0, 6)), 6)
                dve.wait_ge(s_step, at_qhi)
                at_qlo = done(dve.tensor_tensor(rows(13, 14).bitcast(F32R), s_norm[:], rows(12, 13),
                                                ALU.subtract), 7)
                done(dve.tensor_scalar(rows(0, 6, True), rows(0, 6), -2.0, None, ALU.mult), 8)
                done(dve.tensor_scalar(rows(6, 9, True), rows(3, 6), -2.0, None, ALU.mult), 9)
                done(dve.tensor_scalar(rows(9, 12, True), rows(0, 3), -2.0, None, ALU.mult), 10)
                dve.wait_ge(s_step, at_qlo)
                dve.tensor_copy(rows(14, 16, True), rows(12, 14)).then_inc(aug_set, 1)

            def add_m1_m2(n, p):
                dve.wait_ge(m2_set, n + 1)
                dve.tensor_tensor(ab[:, 0, :], ps_c[:, 0:T], m2_f[:], ALU.add)
                dve.tensor_tensor(ab[:, 1, :], ps_c[:, 0:T], m2_f[:], ALU.subtract).then_inc(m1_used, 1)
                dve.wait_ge(m1_used, n + 1)
                dve.scalar_tensor_tensor(out=ab[:], in0=ab[:], scalar=dv[:, SC2:SC2 + 1],
                                         in1=x_f[p][:].rearrange("p (t q) -> p q t", q=2),
                                         op0=ALU.mult, op1=ALU.add).then_inc(ab_set, 1)

            def add_m0_or_m3(n, odd):
                dve.wait_ge((m0_ready, m3_ready)[odd], n + 1)
                dve.wait_ge(ab_set, n + 1)
                dve.scalar_tensor_tensor(out=ab[:, odd, :], in0=ps_c[:, odd * T:(odd + 1) * T],
                                         scalar=dv[:, SC2:SC2 + 1], in1=ab[:, odd, :],
                                         op0=ALU.mult, op1=ALU.add).then_inc(c_sum_set[odd], 1)

            def c_odd_low(n):
                dve.wait_ge(c_hi_set, 2 * (n + 1))
                dve.tensor_tensor(c_lo[:, 1::2], c_f[:], c_hi[:, 1::2].bitcast(F32),
                                  ALU.subtract).then_inc(c_odd_lo_set, 1)

            def n_low(n):
                dve.wait_ge(n_hi_set, n + 1)
                dve.tensor_tensor(n_lo[:], ps_n[:], n_hi[:].bitcast(F32), ALU.subtract).then_inc(n_lo_set, 1)

            def reset_n(g):
                dve.wait_ge(r_act, g + 1)
                dve.scalar_tensor_tensor(out=g_n, in0=g_r, scalar=1.0, in1=g_n, op0=ALU.add,
                                         op1=ALU.mult).then_inc(rn_set, 1)

            def pre_n(g):
                dve.wait_ge(in_ready, g + 1)
                dve.wait_ge(rn_set, g + 1)
                dve.tensor_tensor(g_r, ps_m[:], g_n, ALU.add).then_inc(pre_n_set, 1)

            def blend_x(g):
                dve.wait_ge(z_act, g + 1)
                dve.wait_ge(pre_n_set, g + 1)
                dve.wait_ge(xg_in, 16 * (g + 1))
                dve.scalar_tensor_tensor(out=g_n, in0=g_z, scalar=3.0, in1=x_gate[:], op0=ALU.add,
                                         op1=ALU.mult).then_inc(p_set, 1)

            def blend_n(g):
                dve.wait_ge(n_act, g + 1)
                dve.wait_ge(p_set, g + 1)
                dve.scalar_tensor_tensor(out=g_z, in0=g_z, scalar=-1.0, in1=g_r, op0=ALU.add,
                                         op1=ALU.mult).then_inc(q_set, 1)

            def blend(g):
                dve.wait_ge(q_set, g + 1)
                dve.tensor_tensor(g_n, g_n, g_z, ALU.subtract).then_inc(y_set, 1)

            NORM_STEPS = 6

            def norm_stats(g):
                dve.wait_ge(yT_ready, g + 1)
                for c in range(NC):
                    ins = dve.bn_stats(stats[:, c, :], ps_m[:, c * P:(c + 1) * P])
                ins.then_inc(stats_set, 1)
                me, qe, mo, qo = (stats[:, :, k] for k in (1, 2, 4, 5))
                half = P // 2
                dve.wait_ge(stats_set, g + 1)
                dve.tensor_tensor(norm_d[:], me, mo, ALU.subtract).then_inc(norm_step, 1)
                dve.tensor_tensor(norm_m[:], me, mo, ALU.add).then_inc(norm_step, 1)
                dve.tensor_tensor(norm_q[:], qe, qo, ALU.add).then_inc(norm_step, 1)
                dve.wait_ge(norm_step, NORM_STEPS * g + 2)
                dve.tensor_tensor(norm_d[:], norm_d[:], norm_d[:], ALU.mult).then_inc(norm_step, 1)
                dve.tensor_scalar(norm_m[:], norm_m[:], 0.5, None, ALU.mult).then_inc(norm_step, 1)
                dve.wait_ge(norm_step, NORM_STEPS * g + 4)
                dve.scalar_tensor_tensor(out=norm_q[:], in0=norm_d[:], scalar=half / 2, in1=norm_q[:],
                                         op0=ALU.mult, op1=ALU.add).then_inc(norm_step, 1)
                dve.wait_ge(norm_step, NORM_STEPS * g + 6)
                dve.tensor_scalar(rstd[:], norm_q[:], 1.0 / P, 4 * EPS, ALU.mult, ALU.add).then_inc(var_set, 1)

            def norm_apply(g, half):
                if half == 0:
                    dve.wait_ge(rstd_set, g + 1)
                for c in range(half * NC // 2, (half + 1) * NC // 2):
                    ins = dve.tensor_scalar(y_out[:, c, :], ps_m[:, c * P:(c + 1) * P],
                                            norm_m[:, c:c + 1], rstd[:, c:c + 1], ALU.subtract, ALU.mult)
                if half:
                    ins.then_inc(normed, 1)

            def batch(b, p, first, last):
                for c in range(NC):
                    mask(b, c)
                    if c == 0 and not first:
                        add_m0_or_m3(b - 1, 1)
                    if c == 2 and not first:
                        reset_n(b - 1)
                    if c == 5 and not first:
                        blend(b - 1)
                    if c == 6 and not last:
                        msg_low(b + 1, 1 - p)
                    if c == 7 and not first:
                        norm_apply(b - 1, 0)
                    a_low(b, c)
                    if c == 0 and not first:
                        n_low(b - 1)
                        c_odd_low(b - 1)
                    if c == 3 and not first:
                        pre_n(b - 1)
                        blend_x(b - 1)
                    if c == 4:
                        if not first:
                            blend_n(b - 1)
                        add_m1_m2(b, p)
                    if c == 5 and not last:
                        messages_and_s(b + 1, True)
                        score_rows(b + 1)
                    if c == 6:
                        add_m0_or_m3(b, 0)
                        if not first:
                            norm_stats(b - 1)
                    if c == 7 and not first:
                        norm_apply(b - 1, 1)

            dve.memset(h_f[:, 0:PAD], 0.0)
            dve.memset(h_f[:, PAD + N:], 0.0).then_inc(pads_set, 1)
            dve.memset(s_aug[:], 0.0).then_inc(se_zero, 1)
            dve.wait_ge(se_zero, 1)
            dve.memset(s_aug[:, :, 14:16], 1.0)
            dve.memset(s_aug[:, :, ROFF + 12:ROFF + 14], 1.0)
            dve.memset(bse[:, :, 3:4], 0.0)
            dve.memset(w_f[:, W_SE + 3:W_SE + 4], 0.0).then_inc(se_zero, 1)
            dve.memset(norm_d[:], 0.0).then_inc(normed, 1)
            dve.memset(norm_m[:], 0.0).then_inc(y_out_free, 16)

            def split_conv_weights():
                def taps(k, n):
                    return w_f[:, W_C2 + k * P:].rearrange("p (g n) -> p g n", n=P)[:, 0:3 * n - 2:3, :]

                def used(w, m, n):
                    return w[:, W_U[m]:W_U[m] + n * P].rearrange("p (g n) -> p g n", n=P)

                u1, u2 = u_f[:, 0:GROUPS * P], u_f[:, GROUPS * P:2 * GROUPS * P]
                v1, v2 = (u.rearrange("p (g n) -> p g n", n=P) for u in (u1, u2))
                dve.tensor_tensor(v1[:, 0:FULL, :], taps(0, FULL), taps(2, FULL), ALU.add).then_inc(w_step, 1)
                dve.tensor_copy(v1[:, FULL:, :], taps(0, GROUPS)[:, FULL:, :]).then_inc(w_step, 1)
                dve.wait_ge(w_step, 2)
                dve.tensor_tensor(v2, v1, taps(1, GROUPS), ALU.subtract).then_inc(w_step, 1)
                dve.wait_ge(w_step, 3)
                dve.tensor_tensor(v1, v1, taps(1, GROUPS), ALU.add).then_inc(w_step, 1)
                dve.wait_ge(w_step, 4)
                dve.tensor_scalar(u_f, u_f, 0.5, None, ALU.mult).then_inc(w_step, 1)
                dve.wait_ge(w_step, 5)
                dve.tensor_copy(w_hi[:, W_U[1]:W_U[3]], u_f)
                dve.tensor_copy(used(w_hi, 0, GROUPS), taps(0, GROUPS))
                dve.tensor_scalar(used(w_hi, 3, FULL), taps(2, FULL), -1.0, None, ALU.mult).then_inc(w_step, 1)
                dve.wait_ge(w_step, 6)
                dve.tensor_tensor(w_lo[:, W_U[1]:W_U[3]], u_f, w_hi[:, W_U[1]:W_U[3]].bitcast(F32), ALU.subtract)
                dve.tensor_tensor(used(w_lo, 0, GROUPS), taps(0, GROUPS), used(w_hi, 0, GROUPS).bitcast(F32),
                                  ALU.subtract)
                dve.scalar_tensor_tensor(out=used(w_lo, 3, FULL), in0=taps(2, FULL), scalar=-1.0,
                                         in1=used(w_hi, 3, FULL).bitcast(F32), op0=ALU.mult,
                                         op1=ALU.subtract).then_inc(w_lo_set, 1)

            def split_weights(w0, w1, k):
                dve.tensor_copy(w_hi[:, w0:w1], w_f[:, w0:w1]).then_inc(w_hi_set, 1)
                dve.wait_ge(w_hi_set, k)
                dve.tensor_tensor(w_lo[:, w0:w1], w_f[:, w0:w1], w_hi[:, w0:w1].bitcast(F32),
                                  ALU.subtract).then_inc(w_lo_set, 1)

            dve.wait_ge(se_zero, 2)
            dve.wait_ge(w_first_in, 16 * 3)
            split_weights(W_C1, W_SE + SOFF, 1)
            dve.wait_ge(v_in, 16 * (2 + NC))
            dve.tensor_scalar(bn_var[:], vecs[:, V1:V2 + 1:V2 - V1], EPS, None, ALU.add).then_inc(bn_eps, 1)
            dve.wait_ge(bn_rstd, 1)
            for k, (g, b, m, sc, sh) in enumerate(((G1, B1, M1, SC1, SH1), (G2, B2, M2, SC2, SH2))):
                dve.tensor_tensor(dv[:, sc:sc + 1], vecs[:, g:g + 1], bn_var[:, k:k + 1],
                                  ALU.mult).then_inc(dv_step, 1)
                dve.wait_ge(dv_step, 2 * k + 1)
                dve.tensor_tensor(bn_var[:, k:k + 1], vecs[:, m:m + 1], dv[:, sc:sc + 1],
                                  ALU.mult).then_inc(dv_step, 1)
                dve.wait_ge(dv_step, 2 * k + 2)
                dve.tensor_tensor(dv[:, sh:sh + 1], vecs[:, b:b + 1], bn_var[:, k:k + 1], ALU.subtract)
            dve.tensor_tensor(dv[:, HB_R:HB_Z + 1], vecs[:, BI_R:BI_Z + 1], vecs[:, BH_R:BH_Z + 1],
                              ALU.add).then_inc(dv_step, 1)
            dve.wait_ge(dv_step, 5)
            dve.tensor_scalar(dv[:, HB_R:HB_Z + 1], dv[:, HB_R:HB_Z + 1], 0.5, None, ALU.mult)
            dve.tensor_scalar(dv[:, HB_N:HB_N + 1], vecs[:, BH_N:BH_N + 1], 0.5, None,
                              ALU.mult).then_inc(dv_set, 1)
            messages_and_s(0, False)
            score_rows(0)
            msg_low(0, 0)
            dve.wait_ge(w_rest_in, 16 * 4)
            split_weights(W_HH, W_C2, 2)
            split_conv_weights()
            runs(dve, batch)
            add_m0_or_m3(B - 1, 1)
            c_odd_low(B - 1)
            n_low(B - 1)
            reset_n(B - 1)
            pre_n(B - 1)
            blend_x(B - 1)
            blend_n(B - 1)
            blend(B - 1)
            norm_stats(B - 1)
            norm_apply(B - 1, 0)
            norm_apply(B - 1, 1)

        @block.gpsimd
        def _(pool):
            pool.memset(neg_half[:], -0.5).then_inc(consts_set, 1)
            pool.memset(ident[:], 0.0).then_inc(ident_zero, 1)
            pool.wait_ge(ident_zero, 1)
            pool.affine_select(out=ident[:], in_=ident[:], compare_op=ALU.not_equal, fill=1.0, base=0,
                               pattern=[[-1, P]], channel_multiplier=1).then_inc(ident_set, 1)
            pool.wait_ge(consts_set, 1)
            pool.wait_ge(bn_eps, 1)
            pool.tensor_tensor(bn_var[:], bn_var[:], neg_half[:, 0:2], ALU.pow).then_inc(bn_rstd, 1)

            def norm_scale(g):
                pool.wait_ge(var_set, g + 1)
                pool.tensor_tensor(rstd[:], rstd[:], neg_half[:], ALU.pow).then_inc(rstd_set, 1)

            def x_low(n, p):
                pool.wait_ge(x_hi_set, n + 1)
                pool.tensor_tensor(x_lo[p][:], x_f[p][:], x_hi[p][:].bitcast(F32),
                                   ALU.subtract).then_inc(x_lo_set, 1)

            def differences(n, d):
                if d == 1:
                    pool.wait_ge(h_f_set, n + 1)
                if d == 2:
                    pool.wait_ge(d_lo_set[1], n + 1)
                if d == 0:
                    pool.wait_ge(d_lo_set[2], n + 1)
                a, z, op = ((0, 2, ALU.subtract), (1, 2, ALU.add), (2, 1, ALU.subtract))[d]
                at = [h_f[:, k:k + 2 * DW].rearrange("p (t q) -> p q t", q=2) for k in (a, z)]
                pool.tensor_tensor(d_f[:], at[0], at[1], op).then_inc(d_f_set[d], 1)

            def d_low(n, d):
                pool.wait_ge(d_hi_set[d], n + 1)
                pool.tensor_tensor(d_lo[d][:], d_f[:], d_hi[d][:].bitcast(F32),
                                   ALU.subtract).then_inc(d_lo_set[d], 1)

            def c_even_low(n):
                pool.wait_ge(c_hi_set, 2 * n + 1)
                pool.tensor_tensor(c_lo[:, 0::2], c_f[:], c_hi[:, 0::2].bitcast(F32),
                                   ALU.subtract).then_inc(c_even_lo_set, 1)

            def batch(b, p, first, last):
                differences(b, 2)
                d_low(b, 2)
                differences(b, 0)
                d_low(b, 0)
                if not last:
                    x_low(b + 1, 1 - p)
                    differences(b + 1, 1)
                    d_low(b + 1, 1)
                if not first:
                    norm_scale(b - 1)
                c_even_low(b)

            x_low(0, 0)
            pool.wait_ge(pads_set, 1)
            differences(0, 1)
            d_low(0, 1)
            runs(pool, batch)
            norm_scale(B - 1)


_ORDER = ["xT", "adjT", "w_c1", "w_msg", "w_se", "w_hh", "w_ih", "w_c2", "vec", "b_msg", "b_se"]


def kernel(**inputs):
    import numpy as np
    import concourse.bacc as bacc
    from concourse.bass_utils import run_bass_kernel_spmd

    a = {k.replace("L0_gnn_", ""): np.asarray(v) for k, v in inputs.items()}
    d = a["x"].shape[-1]
    arrays = {
        "xT": a["x"].transpose(0, 2, 1),
        "adjT": a["adj"].transpose(0, 2, 1),
        "w_c1": a["conv1_w"][:, :, 0].T,
        "w_msg": a["w_msg"].T,
        "w_se": a["w_se"].T,
        "w_hh": a["w_hh"].T,
        "w_ih": a["w_ih"].T,
        "w_c2": a["conv2_w"].transpose(1, 2, 0).reshape(d, -1),
        "vec": np.stack([a["bn1_g"], a["bn1_b"], a["bn1_m"], a["bn1_v"],
                         a["bn2_g"], a["bn2_b"], a["bn2_m"], a["bn2_v"],
                         *a["b_ih"].reshape(3, d), *a["b_hh"].reshape(3, d)], axis=1),
        "b_msg": a["b_msg"],
        "b_se": a["b_se"],
    }
    arrays = {k: np.ascontiguousarray(v) for k, v in arrays.items()}
    nc = bacc.Bacc("TRN2", target_bir_lowering=False, num_devices=1)
    args = [nc.dram_tensor(f"{n}_in", arrays[n].shape, F32, kind="ExternalInput").ap() for n in _ORDER]
    out = nc.dram_tensor("out", a["x"].shape, F32, kind="ExternalOutput").ap()
    build(nc, *args, out)
    r = run_bass_kernel_spmd(nc, [{f"{n}_in": arrays[n] for n in _ORDER}], core_ids=[0])
    return r.results[0]["out"]
```

```python
from contextlib import ExitStack

import concourse.bass as bass
from concourse import mybir

F32 = mybir.dt.float32
F32R = mybir.dt.float32r
ALU = mybir.AluOpType
ACT = mybir.ActivationFunctionType
AX = mybir.AxisListType

P = 128
TAPS = 17
PAD = TAPS // 2
GROUPS = -(-TAPS // 3)
FULL = TAPS // 3
EPS = 1e-5
KROWS = 16
QUAD = 32
SOFF = 4
BANK = 512
WARM_UP = 22

W_C1 = 0
W_MSG = W_C1 + P
W_SE = W_MSG + P
W_HH = W_SE + SOFF
W_IHC = W_HH + 3 * P
W_IHN = W_IHC + 3 * P
W_C2 = W_IHN + 3 * P
W_RAW = W_C2 + TAPS * P
W_U = [W_C2 + k * GROUPS * P for k in range(4)]
W_ALL = W_U[3] + FULL * P

(G1, B1, M1, V1, G2, B2, M2, V2, BI_R, BI_Z, BI_N, BH_R, BH_Z, BH_N) = range(14)
(SC1, SH1, SC2, SH2, HB_R, HB_Z, HB_N) = range(7)


def build(nc, xT, adjT, w_c1, w_msg, w_se, w_hh, w_ih, w_c2, vec, b_msg, b_se, out):
    B, D, N = xT.shape
    NC = N // P
    HALVES = N // BANK
    SLOTS = 4
    LPB = NC // SLOTS
    T = N // 2
    DW = (N + 2 * PAD - 2) // 2

    with ExitStack() as ctx:
        def sb(name, shape, dt=F32):
            return ctx.enter_context(nc.sbuf_tensor(name, shape, dt))

        def pb(name, shape):
            return ctx.enter_context(nc.psum_tensor(name, shape, F32))

        def sem(name):
            return ctx.enter_context(nc.semaphore(name))

        w_hi = sb("w_hi", [P, W_ALL], F32R)
        w_lo = sb("w_lo", [P, W_ALL], F32R)
        vecs = sb("vecs", [P, 14])
        dv = sb("dv", [P, 7])
        bmsg = sb("bmsg", [P, P])
        bse = sb("bse", [P, SOFF])
        ident = sb("ident", [P, P])
        bn_var = sb("bn_var", [P, 2])
        neg_half = sb("neg_half", [P, NC])
        adj_ring = sb("adj_ring", [P, SLOTS, N])
        x_f = [sb(f"x_f{p}", [P, N]) for p in range(2)]
        x_hi = [sb(f"x_hi{p}", [P, N], F32R) for p in range(2)]
        x_lo = [sb(f"x_lo{p}", [P, N], F32R) for p in range(2)]
        x_gate = sb("x_gate", [P, N])
        h_f = sb("h_f", [P, N + 2 * PAD])
        d_f = sb("d_f", [P, 2, DW])
        d_hi = [sb(f"d_hi{k}", [P, 2, DW], F32R) for k in range(3)]
        d_lo = [sb(f"d_lo{k}", [P, 2, DW], F32R) for k in range(3)]
        msg_hi = [sb(f"msg_hi{p}", [P, N], F32R) for p in range(2)]
        msg_lo = [sb(f"msg_lo{p}", [P, N], F32R) for p in range(2)]
        a_f = [sb(f"a_f{k}", [P, N]) for k in range(2)]
        a_hi = [sb(f"a_hi{p}", [P, N], F32R) for p in range(2)]
        a_lo = [sb(f"a_lo{p}", [P, N], F32R) for p in range(2)]
        m2_f = sb("m2_f", [P, T])
        ab = sb("ab", [P, 2, T])
        c_f = sb("c_f", [P, T])
        c_hi = sb("c_hi", [P, N], F32R)
        c_lo = sb("c_lo", [P, N], F32R)
        n_hi = sb("n_hi", [P, N], F32R)
        n_lo = sb("n_lo", [P, N], F32R)
        score_l = sb("score_l", [KROWS, N], F32R)
        score_r = sb("score_r", [KROWS, N], F32R)
        s_f = sb("s_f", [P, NC, SOFF])
        s_sq = sb("s_sq", [P, NC, SOFF])
        s_norm = sb("s_norm", [P, NC, 1])
        s_aug = sb("s_aug", [P, NC // 2, 2, 2, QUAD])
        gates = sb("gates", [P, N + max(2 * N, W_RAW)])
        w_f = gates[:, N:N + W_RAW]
        g_r = gates[:, 0:N]
        g_z = gates[:, N:2 * N]
        g_n = gates[:, 2 * N:3 * N]
        msg_f = g_r
        y_out = g_z.rearrange("p (c d) -> p c d", c=NC)
        u1 = adj_ring[:, SLOTS - 1, 0:GROUPS * P]
        u2 = x_gate[:, 0:GROUPS * P]
        stats = sb("stats", [P, NC, 6])
        norm_d = sb("norm_d", [P, NC])
        norm_m = sb("norm_m", [P, NC])
        norm_q = sb("norm_q", [P, NC])
        rstd = sb("rstd", [P, NC])
        shift = sb("shift", [P, NC])

        ps_s = pb("ps_s", [P, N])
        ps_n = pb("ps_n", [P, N])
        ps_c = pb("ps_c", [P, N])
        ps_m = pb("ps_m", [P, N])

        def taps(k, n):
            return w_f[:, W_C2 + k * P:].rearrange("p (g n) -> p g n", n=P)[:, 0:3 * n - 2:3, :]

        def used(w, m, n):
            return w[:, W_U[m]:W_U[m] + n * P].rearrange("p (g n) -> p g n", n=P)

        z_last = ab[:].rearrange("p q t -> p (q t)")
        half = [slice(h * N // 2, (h + 1) * N // 2) for h in range(2)]

        CPB = BANK // (P + SOFF)

        def by_node_out(c, a, z):
            ps, c = (ps_m, c) if c < 2 * CPB else (ps_s, c - 2 * CPB)
            at = c // CPB * BANK + c % CPB * (P + SOFF)
            return ps[:, at + a:at + z]

        def by_node_in_m(a, z):
            banks = ps_m[:].rearrange("p (h n) -> p h n", h=2)[:, :, 0:CPB * (P + SOFF)]
            return banks.rearrange("p h (c n) -> p h c n", c=CPB)[:, :, :, a:z]

        def by_node_in_s(a, z):
            rest = ps_s[:, 0:(NC - 2 * CPB) * (P + SOFF)]
            return rest.rearrange("p (c n) -> p c n", n=P + SOFF)[:, :, a:z]

        w_first_in = sem("w_first_in"); w_conv_in = sem("w_conv_in"); w_gates_in = sem("w_gates_in"); v_in = sem("v_in"); x_in = sem("x_in"); xg_in = sem("xg_in")
        adj_in = [sem(f"adj_in{q}") for q in range(SLOTS)]
        y_out_free = sem("y_out_free")
        ident_zero = sem("ident_zero"); ident_set = sem("ident_set")
        w_hi_set = sem("w_hi_set"); w_lo_set = sem("w_lo_set"); w_step = sem("w_step"); se_zero = sem("se_zero")
        w_gates_hi_set = sem("w_gates_hi_set"); w_gates_lo_set = sem("w_gates_lo_set")
        w_g0_hi_set = sem("w_g0_hi_set"); w_g0_lo_set = sem("w_g0_lo_set")
        consts_set = sem("consts_set"); bn_eps = sem("bn_eps"); bn_rstd = sem("bn_rstd")
        dv_step = sem("dv_step"); dv_set = sem("dv_set"); pads_set = sem("pads_set")
        scores_ready = sem("scores_ready"); nmp_done = sem("nmp_done"); m1_ready = sem("m1_ready"); m2_ready = sem("m2_ready")
        m0_ready = sem("m0_ready"); m3_ready = sem("m3_ready")
        r_ready = sem("r_ready"); z_ready = sem("z_ready"); hn_ready = sem("hn_ready")
        in_ready = sem("in_ready"); conv1_ready = sem("conv1_ready"); by_node_ready = sem("by_node_ready")
        aug_ready = sem("aug_ready"); yT_ready = sem("yT_ready")
        d_hi_set = [sem(f"d_hi_set{k}") for k in range(3)]
        exp_done = sem("exp_done"); a_hi_set = sem("a_hi_set"); x_hi_set = sem("x_hi_set")
        h_f_set = sem("h_f_set"); m2_set = sem("m2_set"); msg_hi_set = sem("msg_hi_set")
        c_f_set = sem("c_f_set"); c_hi_set = sem("c_hi_set"); n_hi_set = sem("n_hi_set")
        operands_set = sem("operands_set"); r_act = sem("r_act"); z_act = sem("z_act"); hn_act = sem("hn_act")
        n_act = sem("n_act")
        masked = sem("masked"); a_lo_set = sem("a_lo_set"); x_m2_set = sem("x_m2_set")
        ab_set = sem("ab_set"); d_f_set = [sem(f"d_f_set{k}") for k in range(3)]; msg_f_set = sem("msg_f_set"); msg_lo_set = sem("msg_lo_set")
        c_sum_set = [sem("c_even_set"), sem("c_odd_set")]; n_lo_set = sem("n_lo_set")
        s_f_set = sem("s_f_set"); ps_s_left = sem("ps_s_left"); s_step = sem("s_step"); aug_set = sem("aug_set")
        rn_set = sem("rn_set"); pre_n_set = sem("pre_n_set")
        p_set = sem("p_set"); q_set = sem("q_set"); y_set = sem("y_set"); stats_set = sem("stats_set")
        norm_step = sem("norm_step"); var_set = sem("var_set"); normed = [sem("normed0"), sem("normed1")]
        x_lo_set = sem("x_lo_set"); d_lo_set = [sem(f"d_lo_set{k}") for k in range(3)]
        c_lo_set = [sem("c_even_lo_set"), sem("c_odd_lo_set")]
        rstd_set = sem("rstd_set"); shift_set = sem("shift_set")

        block = ctx.enter_context(nc.Block())

        def runs(eng, batch):
            batch(0, 0, True, False)
            with eng.Fori(0, (B - 2) // 2) as i:
                batch(i * 2 + 1, 1, False, False)
                batch(i * 2 + 2, 0, False, False)
            batch(B - 1, (B - 1) % 2, False, True)

        @block.sync
        def _(sp):
            def load_x(b, p):
                sp.dma_start(x_f[p][:], xT[b]).then_inc(x_in, 16)

            def load_adj(b, c):
                sp.dma_start(adj_ring[:, c % SLOTS, :],
                             adjT[b, c * P:(c + 1) * P, :]).then_inc(adj_in[c % SLOTS], 16)

            load_x(0, 0)
            sp.dma_start(w_f[:, W_C1:W_C1 + P], w_c1).then_inc(w_first_in, 16)
            sp.dma_start(w_f[:, W_MSG:W_MSG + P], w_msg).then_inc(w_first_in, 16)
            sp.dma_start(w_f[:, W_SE:W_SE + 3], w_se).then_inc(w_first_in, 16)
            sp.dma_start(vecs[:], vec).then_inc(v_in, 16)
            sp.dma_start(bmsg[:], b_msg.partition_broadcast(P)).then_inc(v_in, 16)
            sp.dma_start(bse[:, 0:3], b_se.partition_broadcast(P)).then_inc(v_in, 16)
            sp.dma_start(w_f[:, W_C2:W_RAW], w_c2).then_inc(w_conv_in, 16)
            load_adj(0, 0)
            load_adj(0, 1)
            sp.dma_start(w_f[:, W_HH:W_HH + 3 * P], w_hh).then_inc(w_gates_in, 16)
            sp.dma_start(w_f[:, W_IHC:W_IHC + 3 * P], w_ih[0:P, :]).then_inc(w_gates_in, 16)
            sp.dma_start(w_f[:, W_IHN:W_IHN + 3 * P], w_ih[P:2 * P, :]).then_inc(w_gates_in, 16)
            load_adj(0, 2)
            sp.wait_ge(w_lo_set, 3)
            load_adj(0, 3)

            def load_x_gate(g):
                sp.dma_start(x_gate[:], xT[g]).then_inc(xg_in, 16)

            def store(g):
                for h in range(2):
                    sp.wait_ge(normed[h], g + 2)
                    sp.dma_start(out[g, h * N // 2:(h + 1) * N // 2, :].rearrange("(c p) d -> p c d", p=P),
                                 y_out[:, h * NC // 2:(h + 1) * NC // 2, :]).then_inc(y_out_free, 16)

            def batch(b, p, first, last):
                if not last:
                    if not first:
                        sp.wait_ge(ab_set, b)
                    load_x(b + 1, 1 - p)
                if not first:
                    load_x_gate(b - 1)
                for c in range(SLOTS if last else NC):
                    sp.wait_ge(masked, b * NC + c + 1)
                    if c < SLOTS:
                        load_adj(b, c + SLOTS)
                    else:
                        load_adj(b + 1, c - SLOTS)
                if last:
                    sp.wait_ge(p_set, b)
                    load_x_gate(b)
                if not first:
                    store(b - 1)

            runs(sp, batch)
            store(B - 1)
            sp.wait_ge(y_out_free, 16 + 32 * B)

        @block.tensor
        def _(pe):
            def three(outs, w0, w1, rhs_hi, rhs_lo, first, last):
                w_h, w_l = w_hi[:, w0:w1], w_lo[:, w0:w1]
                for lhs, rhs, k in ((w_h, rhs_hi, 0), (w_h, rhs_lo, 1), (w_l, rhs_hi, 2)):
                    for o, r in zip(outs, rhs):
                        mm = pe.matmul(o, lhs, r, start=(first and k == 0), stop=(last and k == 2))
                return mm

            def banks(t, off=0):
                return [t[:, off + h * BANK:off + (h + 1) * BANK] for h in range(HALVES)]

            def scores(b, c):
                if c == 0:
                    pe.wait_ge(operands_set, 4 * (b + 1))
                else:
                    pe.wait_ge(exp_done, b * NC + c)
                for o, r in zip(banks(ps_s), banks(score_r)):
                    mm = pe.matmul(o, score_l[:, c * P:(c + 1) * P], r, start=True, stop=True)
                mm.then_inc(scores_ready, 1)

            def sum_messages(b, p, c, first):
                if c == 0:
                    pe.wait_ge(msg_lo_set, b + 1)
                    if not first:
                        pe.wait_ge(n_lo_set, b)
                pe.wait_ge(a_lo_set, b * NC + c + 1)
                m_h, m_l = (t[p][:, c * P:(c + 1) * P] for t in (msg_hi, msg_lo))
                a_h, a_l = banks(a_hi[c % 2]), banks(a_lo[c % 2])
                for lhs, rhs, k in ((m_h, a_h, 0), (m_h, a_l, 1), (m_l, a_h, 2)):
                    for o, r in zip(banks(ps_n), rhs):
                        mm = pe.matmul(o, lhs, r, start=(c == 0 and k == 0), stop=(c == NC - 1 and k == 2))
                mm.then_inc(nmp_done, 1)

            M2, M1, M3, M0 = (2, 2, 0, GROUPS), (1, 1, 0, GROUPS), (3, 0, 1, FULL), (0, 0, 0, GROUPS)
            conv_passes = [(m, d, at + 3 * g, g, s, g == 0 and s == 0, g == n - 1 and s == 2)
                           for m, d, at, n in (M2, M1, M3, M0) for g in range(n) for s in range(3)]
            ALL = len(conv_passes)
            conv_steps = ((7, 14), (15, 15), (17, 17), (24, 24), (30, 37), (37, 43), (49, 56), (62, ALL))
            conv_steps_first = ((9, 18), (26, 26), (34, 34), (40, 40), (44, 48), (48, 51), (55, 60), (64, ALL))
            BEFORE_SCORES = 6
            bank_of = {1: 0, 2: 1, 0: 0, 3: 1}
            weights_of = {2: (w_lo_set, 2), 1: (w_lo_set, 3), 3: (w_lo_set, 4), 0: (w_g0_lo_set, 1)}

            def conv2(b, n0, n1, first):
                for n in range(n0, n1):
                    m, d, i, g, s, begins, ends = conv_passes[n]
                    if begins:
                        if first:
                            pe.wait_ge(*weights_of[m])
                        if m != 0:
                            pe.wait_ge(d_lo_set[d], b + 1)
                        if m == 2 and not first:
                            pe.wait_ge(c_sum_set[1], b)
                        if m == 1 and not first:
                            pe.wait_ge(c_sum_set[0], b)
                        if m == 3:
                            pe.wait_ge(m2_set, b + 1)
                        if m == 0:
                            pe.wait_ge(ab_set, b + 1)
                    w = (w_lo if s == 2 else w_hi)[:, W_U[m] + g * P:W_U[m] + (g + 1) * P]
                    h = (d_lo if s == 1 else d_hi)[d][:, i % 2, i // 2:i // 2 + T]
                    mm = pe.matmul(ps_c[:, bank_of[m] * T:(bank_of[m] + 1) * T], w, h, start=begins, stop=ends)
                    if ends:
                        mm.then_inc((m0_ready, m1_ready, m2_ready, m3_ready)[m], 1)

            def conv1(n, p):
                pe.wait_ge(x_lo_set, n + 1)
                three(banks(ps_m), W_C1, W_C1 + P, banks(x_hi[p]), banks(x_lo[p]),
                      True, True).then_inc(conv1_ready, 1)

            def by_node(n, p, left_s):
                for c in range(NC):
                    if c == 2 * CPB and left_s is not None:
                        pe.wait_ge(exp_done, left_s)
                    o = by_node_out(c, 0, P + SOFF)
                    for k, (x, w) in enumerate(((x_hi, w_hi), (x_hi, w_lo), (x_lo, w_hi))):
                        mm = pe.matmul(o, x[p][:, c * P:(c + 1) * P], w[:, W_MSG:W_MSG + P + SOFF],
                                       start=(k == 0), stop=(k == 2))
                mm.then_inc(by_node_ready, 1)

            def score_operands(n):
                pe.wait_ge(aug_set, n + 1)
                for c in range(NC // 2):
                    mm = pe.transpose(ps_s[:, c * P:(c + 1) * P],
                                      s_aug[:, c].rearrange("p h q k -> p (h q k)"), ident[:])
                mm.then_inc(aug_ready, 1)

            def gate_hn(g, p):
                for h in range(2):
                    pe.wait_ge(normed[h], g + 1)
                three(banks(ps_m), W_HH + 2 * P, W_HH + 3 * P, banks(x_hi[p]), banks(x_lo[p]),
                      True, True).then_inc(hn_ready, 1)

            def gate_rz(g, p, j, ready):
                three(banks(ps_m), W_HH + j * P, W_HH + (j + 1) * P, banks(x_hi[p]), banks(x_lo[p]),
                      True, False)
                if j == 0:
                    pe.wait_ge(n_lo_set, g + 1)
                three(banks(ps_m), W_IHN + j * P, W_IHN + (j + 1) * P, banks(n_hi), banks(n_lo),
                      False, False)
                if j == 0:
                    pe.wait_ge(c_lo_set[1], g + 1)
                    pe.wait_ge(c_lo_set[0], g + 1)
                three(banks(ps_m), W_IHC + j * P, W_IHC + (j + 1) * P, banks(c_hi), banks(c_lo),
                      False, True).then_inc(ready, 1)

            def gate_r(g, p):
                pe.wait_ge(hn_act, g + 1)
                gate_rz(g, p, 0, r_ready)

            def gate_z(g, p):
                pe.wait_ge(r_act, g + 1)
                gate_rz(g, p, 1, z_ready)

            def gate_in(g):
                pe.wait_ge(z_act, g + 1)
                three(banks(ps_m), W_IHC + 2 * P, W_IHC + 3 * P, banks(c_hi), banks(c_lo), True, False)
                three(banks(ps_m), W_IHN + 2 * P, W_IHN + 3 * P, banks(n_hi), banks(n_lo),
                      False, True).then_inc(in_ready, 1)

            def turn_y(g):
                pe.wait_ge(y_set, g + 1)
                for c in range(NC):
                    mm = pe.transpose(ps_m[:, c * P:(c + 1) * P], g_n[:, c * P:(c + 1) * P], ident[:])
                mm.then_inc(yT_ready, 1)

            def batch(b, p, first, last):
                for c in range(NC):
                    steps = conv_steps_first if first else conv_steps
                    done, (mid, end) = steps[c - 1][1] if c else 0, steps[c]
                    if c == 6 and not last:
                        pe.wait_ge(ps_s_left, b + 2)
                    if first and c == 0:
                        conv2(b, 0, BEFORE_SCORES, True)
                        done = BEFORE_SCORES
                    scores(b, c)
                    conv2(b, done, mid, first)
                    if not first:
                        if c == 0:
                            sum_messages(b - 1, 1 - p, NC - 1, False)
                            gate_hn(b - 1, 1 - p)
                        if c == 1:
                            gate_r(b - 1, 1 - p)
                        if c == 2:
                            gate_z(b - 1, 1 - p)
                        if c == 3:
                            gate_in(b - 1)
                    if c == 4 and not last:
                        if not first:
                            pe.wait_ge(pre_n_set, b)
                        conv1(b + 1, 1 - p)
                    if c == 5 and not last:
                        pe.wait_ge(h_f_set, b + 2)
                        by_node(b + 1, 1 - p, b * NC + c + 1)
                    if c == 6 and not first:
                        if not last:
                            pe.wait_ge(msg_f_set, b + 2)
                        turn_y(b - 1)
                    if c == 7 and not last:
                        pe.wait_ge(exp_done, (b + 1) * NC)
                        score_operands(b + 1)
                    conv2(b, mid, end, first)
                    if c > 0:
                        sum_messages(b, p, c - 1, first)
                if first:
                    pe.wait_ge(w_gates_lo_set, 1)

            pe.wait_ge(ident_set, 1)
            for _ in range(WARM_UP):
                pe.transpose(ps_n[:, 0:P], ident[:], ident[:])
            pe.wait_ge(w_lo_set, 1)
            pe.wait_ge(x_hi_set, 1)
            for w in (w_hi, w_lo):
                for o, r in zip(banks(ps_c), banks(x_hi[0])):
                    pe.matmul(o, w[:, W_C1:W_C1 + P], r, start=(w is w_hi), stop=False)
            pe.wait_ge(x_lo_set, 1)
            for o, r in zip(banks(ps_c), banks(x_lo[0])):
                mm = pe.matmul(o, w_hi[:, W_C1:W_C1 + P], r, start=False, stop=True)
            mm.then_inc(conv1_ready, 1)
            by_node(0, 0, None)
            pe.wait_ge(ps_s_left, 1)
            score_operands(0)
            pe.wait_ge(h_f_set, 1)
            pe.wait_ge(msg_f_set, 1)
            runs(pe, batch)

            g, p = B - 1, (B - 1) % 2
            x_h, x_l = banks(x_hi[p]), banks(x_lo[p])
            c_h, c_l = banks(c_hi), banks(c_lo)
            n_h, n_l = banks(n_hi), banks(n_lo)

            def half_of(ps, w0, rhs_hi, rhs_lo, h, first, last):
                return three(banks(ps)[h:h + 1], w0, w0 + P, rhs_hi[h:h + 1], rhs_lo[h:h + 1], first, last)

            pe.wait_ge(exp_done, B * NC)
            three(banks(ps_s), W_HH, W_HH + P, x_h, x_l, True, False)
            sum_messages(g, p, NC - 1, False)
            pe.wait_ge(c_sum_set[0], B)
            pe.wait_ge(c_sum_set[1], B)
            three(banks(ps_c), W_HH + P, W_HH + 2 * P, x_h, x_l, True, False)
            pe.wait_ge(n_lo_set, B)
            three(banks(ps_s), W_IHN, W_IHN + P, n_h, n_l, False, False)
            three(banks(ps_c), W_IHN + P, W_IHN + 2 * P, n_h, n_l, False, False)
            three(banks(ps_n), W_IHN + 2 * P, W_IHN + 3 * P, n_h, n_l, True, False)
            pe.wait_ge(c_lo_set[0], B)
            pe.wait_ge(c_lo_set[1], B)
            for h in range(2):
                half_of(ps_s, W_IHC, c_h, c_l, h, False, True).then_inc(r_ready, 1)
                pe.wait_ge(normed[h], B)
                half_of(ps_m, W_HH + 2 * P, x_h, x_l, h, True, True).then_inc(hn_ready, 1)
                half_of(ps_c, W_IHC + P, c_h, c_l, h, False, True).then_inc(z_ready, 1)
                half_of(ps_n, W_IHC + 2 * P, c_h, c_l, h, False, True).then_inc(in_ready, 1)
            for h in range(2):
                pe.wait_ge(y_set, B + h)
                for c in range(h * NC // 2, (h + 1) * NC // 2):
                    mm = pe.transpose(ps_m[:, c * P:(c + 1) * P], g_n[:, c * P:(c + 1) * P], ident[:])
                mm.then_inc(yT_ready, 1)

        @block.scalar
        def _(act):
            def exps(b, c, first):
                if not (first and c < 2):
                    act.wait_ge(a_lo_set, b * NC + c - 1)
                act.wait_ge(scores_ready, b * NC + c + 1)
                act.activation(a_f[c % 2][:], ps_s[:], ACT.Exp, scale=-1.0).then_inc(exp_done, 1)

            def a_high(b, c, first):
                if not (first and c < 2):
                    act.wait_ge(nmp_done, b * NC + c - 1)
                act.wait_ge(masked, b * NC + c + 1)
                act.copy(a_hi[c % 2][:], a_f[c % 2][:]).then_inc(a_hi_set, 1)

            def x_high(n, p, reused):
                act.wait_ge(x_in, 16 * (n + 1))
                if reused:
                    act.wait_ge(z_ready, n - 1)
                act.copy(x_hi[p][:], x_f[p][:]).then_inc(x_hi_set, 1)

            def h_full(n, prev, ps):
                act.wait_ge(conv1_ready, n + 1)
                if prev:
                    act.wait_ge(d_lo_set[0], n)
                act.activation(h_f[:, PAD:PAD + N], ps[:], ACT.Relu, bias=dv[:, SH1:SH1 + 1],
                               scale=dv[:, SC1:SC1 + 1]).then_inc(h_f_set, 1)

            def d_high(n, d, prev):
                act.wait_ge(d_f_set[d], n + 1)
                if prev:
                    act.wait_ge((m0_ready, m1_ready, m2_ready)[d], n)
                act.copy(d_hi[d][:], d_f[:]).then_inc(d_hi_set[d], 1)

            def copy_m2(n):
                act.wait_ge(m2_ready, n + 1)
                act.activation(m2_f[:], ps_c[:, T:2 * T], ACT.Identity,
                               scale=dv[:, SC2:SC2 + 1]).then_inc(m2_set, 1)

            def msg_high(n, p, reused):
                act.wait_ge(msg_f_set, n + 1)
                if reused:
                    act.wait_ge(nmp_done, (n - 1) * NC)
                act.activation(msg_hi[p][:], msg_f, ACT.Relu).then_inc(msg_hi_set, 1)

            def both_operands(n):
                act.wait_ge(aug_ready, n + 1)
                for h in range(2):
                    for q, operand in enumerate((score_l, score_r)):
                        row = (2 * h + q) * QUAD
                        act.copy(operand[:, h * N // 2:(h + 1) * N // 2],
                                 ps_s[row:row + KROWS, 0:N // 2]).then_inc(operands_set, 1)

            def c_high(n, odd, prev):
                act.wait_ge(c_sum_set[odd], n + 1)
                if not odd:
                    act.wait_ge(c_lo_set[1], n + 1)
                elif prev:
                    act.wait_ge(c_lo_set[0], n)
                    act.wait_ge(in_ready, n)
                act.activation(c_f[:], ab[:, odd, :], ACT.Relu, bias=dv[:, SH2:SH2 + 1]).then_inc(c_f_set, 1)
                act.activation(c_hi[:, odd::2], ab[:, odd, :], ACT.Relu,
                               bias=dv[:, SH2:SH2 + 1]).then_inc(c_hi_set, 1)

            def n_high(n, prev):
                act.wait_ge(nmp_done, (n + 1) * NC)
                if prev:
                    act.wait_ge(in_ready, n)
                act.copy(n_hi[:], ps_n[:]).then_inc(n_hi_set, 1)

            def act_hn(g):
                act.wait_ge(hn_ready, g + 1)
                act.activation(g_n, ps_m[:], ACT.Identity, bias=dv[:, HB_N:HB_N + 1],
                               scale=0.5).then_inc(hn_act, 1)

            def act_r(g):
                act.wait_ge(r_ready, g + 1)
                act.activation(g_r, ps_m[:], ACT.Tanh, bias=dv[:, HB_R:HB_R + 1],
                               scale=0.5).then_inc(r_act, 1)

            def act_z(g):
                act.wait_ge(z_ready, g + 1)
                act.wait_ge(y_out_free, 16 + 32 * g)
                act.activation(g_z, ps_m[:], ACT.Tanh, bias=dv[:, HB_Z:HB_Z + 1],
                               scale=0.5).then_inc(z_act, 1)

            def act_n(g):
                act.wait_ge(pre_n_set, g + 1)
                act.activation(g_r, g_r, ACT.Tanh, bias=vecs[:, BI_N:BI_N + 1]).then_inc(n_act, 1)

            def norm_apply(g, h):
                act.wait_ge(shift_set, g + 1)
                for c in range(h * NC // 2, (h + 1) * NC // 2):
                    ins = act.activation(y_out[:, c, :], ps_m[:, c * P:(c + 1) * P], ACT.Identity,
                                         bias=shift[:, c:c + 1], scale=rstd[:, c:c + 1])
                ins.then_inc(normed[h], 1)

            def batch(b, p, first, last):
                for c in range(NC):
                    exps(b, c, first)
                    if c == 0 and first:
                        d_high(b, 1, False)
                    if c == 0 and not first:
                        n_high(b - 1, True)
                        act_hn(b - 1)
                    if c == 4 and first:
                        h_full(b + 1, True, ps_m)
                    if c == 4 and not first:
                        act_n(b - 1)
                    if c == 6 and not last:
                        msg_high(b + 1, 1 - p, not first)
                    if c == 7 and not last:
                        both_operands(b + 1)
                    a_high(b, c, first)
                    if c == 0 and not first:
                        c_high(b - 1, 0, True)
                    if c == 0 and first:
                        act.wait_ge(w_gates_in, 16 * 3)
                        act.copy(w_hi[:, W_HH:W_C2], w_f[:, W_HH:W_C2]).then_inc(w_gates_hi_set, 1)
                        act.copy(used(w_hi, 0, GROUPS), taps(0, GROUPS)).then_inc(w_g0_hi_set, 1)
                    if c == 1:
                        if first:
                            d_high(b, 0, False)
                            copy_m2(b)
                        else:
                            act_r(b - 1)
                            d_high(b, 1, True)
                    if c == 2:
                        if not first:
                            act_z(b - 1)
                        if not last:
                            x_high(b + 1, 1 - p, not first)
                    if c == 3 and not first:
                        d_high(b, 0, True)
                        copy_m2(b)
                    if c == 4 and not first and not last:
                        h_full(b + 1, True, ps_m)
                    if c == 5 and not last:
                        d_high(b + 1, 2, True)
                    if c == 7 and not last:
                        if not first:
                            norm_apply(b - 1, 1)
                        c_high(b, 1, not first)

            x_high(0, 0, False)
            act.wait_ge(dv_set, 1)
            h_full(0, False, ps_c)
            d_high(0, 2, False)
            msg_high(0, 0, False)
            both_operands(0)
            runs(act, batch)
            n_high(B - 1, True)
            c_high(B - 1, 1, True)
            c_high(B - 1, 0, True)
            norm_apply(B - 2, 1)
            for h in range(2):
                act.wait_ge(r_ready, B + h)
                act.activation(g_r[:, half[h]], ps_s[:, half[h]], ACT.Tanh, bias=dv[:, HB_R:HB_R + 1],
                               scale=0.5).then_inc(r_act, 1)
                act.wait_ge(hn_ready, B + h)
                act.activation(g_n[:, half[h]], ps_m[:, half[h]], ACT.Identity, bias=dv[:, HB_N:HB_N + 1],
                               scale=0.5).then_inc(hn_act, 1)
                act.wait_ge(z_ready, B + h)
                act.activation(z_last[:, half[h]], ps_c[:, half[h]], ACT.Tanh, bias=dv[:, HB_Z:HB_Z + 1],
                               scale=0.5).then_inc(z_act, 1)
                act.wait_ge(pre_n_set, B + h)
                act.activation(g_r[:, half[h]], g_r[:, half[h]], ACT.Tanh,
                               bias=vecs[:, BI_N:BI_N + 1]).then_inc(n_act, 1)
            act.wait_ge(y_out_free, 16 + 32 * (B - 1))
            norm_apply(B - 1, 0)

        @block.vector
        def _(dve):
            def mask(b, c):
                dve.wait_ge(exp_done, b * NC + c + 1)
                dve.wait_ge(adj_in[c % SLOTS], 16 * (b * LPB + c // SLOTS + 1))
                dve.tensor_tensor(a_f[c % 2][:], a_f[c % 2][:], adj_ring[:, c % SLOTS, :],
                                  ALU.mult).then_inc(masked, 1)

            def a_low(b, c):
                dve.wait_ge(a_hi_set, b * NC + c + 1)
                dve.tensor_tensor(a_lo[c % 2][:], a_f[c % 2][:], a_hi[c % 2][:].bitcast(F32),
                                  ALU.subtract).then_inc(a_lo_set, 1)

            def messages_and_s(n, prev, gates_before, s_only=False):
                if prev:
                    dve.wait_ge(aug_set, n)
                if gates_before:
                    dve.wait_ge(q_set, n - 1)
                dve.wait_ge(by_node_ready, n + 1)
                m = 2 * CPB
                msg = msg_f.rearrange("p (c d) -> p c d", c=NC)
                dve.tensor_tensor(msg[:, m:, :], by_node_in_s(0, P),
                                  bmsg[:].unsqueeze(1).to_broadcast([P, NC - m, P]), ALU.add)
                dve.tensor_tensor(s_f[:, m:, :], by_node_in_s(P, P + SOFF),
                                  bse[:].unsqueeze(1).to_broadcast([P, NC - m, SOFF]),
                                  ALU.add).then_inc(ps_s_left, 1)
                dve.tensor_tensor(s_f[:, 0:m, :].rearrange("p (h c) k -> p h c k", h=2),
                                  by_node_in_m(P, P + SOFF),
                                  bse[:].unsqueeze(1).unsqueeze(1).to_broadcast([P, 2, CPB, SOFF]),
                                  ALU.add).then_inc(s_f_set, 1)
                if not s_only:
                    rest_of_messages()

            def rest_of_messages():
                m = 2 * CPB
                msg = msg_f.rearrange("p (c d) -> p c d", c=NC)
                dve.tensor_tensor(msg[:, 0:m, :].rearrange("p (h c) d -> p h c d", h=2), by_node_in_m(0, P),
                                  bmsg[:].unsqueeze(1).unsqueeze(1).to_broadcast([P, 2, CPB, P]),
                                  ALU.add).then_inc(msg_f_set, 1)

            def msg_low(n, p):
                dve.wait_ge(msg_hi_set, n + 1)
                dve.scalar_tensor_tensor(out=msg_lo[p][:], in0=msg_f, scalar=0.0,
                                         in1=msg_hi[p][:].bitcast(F32), op0=ALU.max,
                                         op1=ALU.subtract).then_inc(msg_lo_set, 1)

            STEPS = 10

            def score_rows(n):
                def rows(a, z, right=False):
                    return s_aug[:, :, :, int(right), a:z]

                def by_half(t):
                    return t.rearrange("p (h c) k -> p c h k", h=2)

                def done(ins, k):
                    ins.then_inc(s_step, 1)
                    return n * STEPS + k

                dve.wait_ge(s_f_set, n + 1)
                done(dve.tensor_tensor(s_sq[:], s_f[:], s_f[:], ALU.mult), 1)
                at_hi = done(dve.tensor_copy(rows(0, 3).bitcast(F32R), by_half(s_f[:, :, 0:3])), 2)
                dve.wait_ge(s_step, at_hi)
                at_norm = done(dve.tensor_reduce(s_norm[:], s_sq[:, :, 0:3], AX.X, ALU.add), 3)
                at_lo = done(dve.tensor_tensor(rows(3, 6).bitcast(F32R), by_half(s_f[:, :, 0:3]), rows(0, 3),
                                               ALU.subtract), 4)
                dve.wait_ge(s_step, at_norm)
                at_qhi = done(dve.tensor_copy(rows(12, 13).bitcast(F32R), by_half(s_norm[:])), 5)
                dve.wait_ge(s_step, at_lo)
                done(dve.tensor_copy(rows(6, 12), rows(0, 6)), 6)
                dve.wait_ge(s_step, at_qhi)
                at_qlo = done(dve.tensor_tensor(rows(13, 14).bitcast(F32R), by_half(s_norm[:]), rows(12, 13),
                                                ALU.subtract), 7)
                done(dve.tensor_scalar(rows(0, 6, True), rows(0, 6), -2.0, None, ALU.mult), 8)
                done(dve.tensor_scalar(rows(6, 9, True), rows(3, 6), -2.0, None, ALU.mult), 9)
                done(dve.tensor_scalar(rows(9, 12, True), rows(0, 3), -2.0, None, ALU.mult), 10)
                dve.wait_ge(s_step, at_qlo)
                dve.tensor_copy(rows(14, 16, True), rows(12, 14)).then_inc(aug_set, 1)

            def add_m1(n):
                dve.wait_ge(m1_ready, n + 1)
                dve.wait_ge(x_m2_set, n + 1)
                dve.scalar_tensor_tensor(out=ab[:], in0=ps_c[:, 0:T].unsqueeze(1).to_broadcast([P, 2, T]),
                                         scalar=dv[:, SC2:SC2 + 1], in1=ab[:],
                                         op0=ALU.mult, op1=ALU.add).then_inc(ab_set, 1)

            def add_m0_or_m3(n, odd):
                dve.wait_ge((m0_ready, m3_ready)[odd], n + 1)
                dve.wait_ge(ab_set, n + 1)
                dve.scalar_tensor_tensor(out=ab[:, odd, :], in0=ps_c[:, odd * T:(odd + 1) * T],
                                         scalar=dv[:, SC2:SC2 + 1], in1=ab[:, odd, :],
                                         op0=ALU.mult, op1=ALU.add).then_inc(c_sum_set[odd], 1)

            def c_even_low(n):
                dve.wait_ge(c_hi_set, 2 * (n + 1))
                dve.tensor_tensor(c_lo[:, 0::2], c_f[:], c_hi[:, 0::2].bitcast(F32),
                                  ALU.subtract).then_inc(c_lo_set[0], 1)

            def n_low(n):
                dve.wait_ge(n_hi_set, n + 1)
                dve.tensor_tensor(n_lo[:], ps_n[:], n_hi[:].bitcast(F32), ALU.subtract).then_inc(n_lo_set, 1)

            def reset_n(g):
                dve.wait_ge(r_act, g + 1)
                dve.scalar_tensor_tensor(out=g_n, in0=g_r, scalar=1.0, in1=g_n, op0=ALU.add,
                                         op1=ALU.mult).then_inc(rn_set, 1)

            def pre_n(g):
                dve.wait_ge(in_ready, g + 1)
                dve.wait_ge(rn_set, g + 1)
                dve.tensor_tensor(g_r, ps_m[:], g_n, ALU.add).then_inc(pre_n_set, 1)

            def blend_x(g):
                dve.wait_ge(z_act, g + 1)
                dve.wait_ge(pre_n_set, g + 1)
                dve.wait_ge(xg_in, 16 * (g + 1))
                dve.scalar_tensor_tensor(out=g_n, in0=g_z, scalar=3.0, in1=x_gate[:], op0=ALU.add,
                                         op1=ALU.mult).then_inc(p_set, 1)

            def blend_n(g):
                dve.wait_ge(n_act, g + 1)
                dve.wait_ge(p_set, g + 1)
                dve.scalar_tensor_tensor(out=g_z, in0=g_z, scalar=-1.0, in1=g_r, op0=ALU.add,
                                         op1=ALU.mult).then_inc(q_set, 1)

            NORM_STEPS = 6

            def norm_measure(n, chunks):
                dve.wait_ge(yT_ready, n + 1)
                for c in range(*chunks):
                    ins = dve.bn_stats(stats[:, c, :], ps_m[:, c * P:(c + 1) * P])
                ins.then_inc(stats_set, 1)

            def norm_variance(n, chunks):
                of = slice(*chunks)
                me, qe, mo, qo = (stats[:, of, k] for k in (1, 2, 4, 5))
                d, m, q = norm_d[:, of], norm_m[:, of], norm_q[:, of]
                dve.wait_ge(stats_set, n + 1)
                dve.tensor_tensor(d, me, mo, ALU.subtract).then_inc(norm_step, 1)
                dve.tensor_tensor(m, me, mo, ALU.add).then_inc(norm_step, 1)
                dve.tensor_tensor(q, qe, qo, ALU.add).then_inc(norm_step, 1)
                dve.wait_ge(norm_step, NORM_STEPS * n + 2)
                dve.tensor_tensor(d, d, d, ALU.mult).then_inc(norm_step, 1)
                dve.tensor_scalar(m, m, -0.5, None, ALU.mult).then_inc(norm_step, 1)
                dve.wait_ge(norm_step, NORM_STEPS * n + 4)
                dve.scalar_tensor_tensor(out=q, in0=d, scalar=P / 4, in1=q,
                                         op0=ALU.mult, op1=ALU.add).then_inc(norm_step, 1)
                dve.wait_ge(norm_step, NORM_STEPS * n + 6)
                dve.tensor_scalar(rstd[:, of], q, 1.0 / P, 4 * EPS, ALU.mult, ALU.add).then_inc(var_set, 1)

            def norm_apply(n, h):
                dve.wait_ge(shift_set, n + 1)
                for c in range(h * NC // 2, (h + 1) * NC // 2):
                    ins = dve.tensor_scalar(y_out[:, c, :], ps_m[:, c * P:(c + 1) * P],
                                            rstd[:, c:c + 1], shift[:, c:c + 1], ALU.mult, ALU.add)
                ins.then_inc(normed[h], 1)

            def batch(b, p, first, last):
                for c in range(NC):
                    mask(b, c)
                    if c == 0 and not first:
                        add_m0_or_m3(b - 1, 0)
                        n_low(b - 1)
                    if c == 2 and not first:
                        reset_n(b - 1)
                    if c == 6 and not last:
                        msg_low(b + 1, 1 - p)
                    if c == 7 and not last:
                        add_m0_or_m3(b, 1)
                    if c == 5 and not last:
                        messages_and_s(b + 1, True, not first)
                    a_low(b, c)
                    if c == 0 and not first:
                        c_even_low(b - 1)
                    if c == 3 and not first:
                        pre_n(b - 1)
                        blend_x(b - 1)
                    if c == 4:
                        if not first:
                            blend_n(b - 1)
                        add_m1(b)
                    if c == 5 and not last:
                        score_rows(b + 1)
                    if c == 6 and not first and not last:
                        norm_measure(b - 1, (0, NC))
                        norm_variance(b - 1, (0, NC))
                    if c == 7 and not first and not last:
                        norm_apply(b - 1, 0)

            dve.memset(h_f[:, 0:PAD], 0.0)
            dve.memset(h_f[:, PAD + N:], 0.0).then_inc(pads_set, 1)
            dve.memset(s_aug[:], 0.0).then_inc(se_zero, 1)
            dve.wait_ge(se_zero, 1)
            dve.memset(s_aug[:, :, :, 0, 14:16], 1.0)
            dve.memset(s_aug[:, :, :, 1, 12:14], 1.0)
            dve.memset(bse[:, 3:4], 0.0)
            dve.memset(w_f[:, W_SE + 3:W_SE + 4], 0.0).then_inc(se_zero, 1)
            dve.memset(norm_d[:], 0.0).then_inc(normed[0], 1)
            dve.memset(norm_m[:], 0.0).then_inc(normed[1], 1)
            dve.memset(norm_q[:], 0.0).then_inc(y_out_free, 16)

            def split_weights(w0, w1, k):
                dve.tensor_copy(w_hi[:, w0:w1], w_f[:, w0:w1]).then_inc(w_hi_set, 1)
                dve.wait_ge(w_hi_set, k)
                dve.tensor_tensor(w_lo[:, w0:w1], w_f[:, w0:w1], w_hi[:, w0:w1].bitcast(F32),
                                  ALU.subtract).then_inc(w_lo_set, 1)

            def sum_taps():
                v1, v2 = (u.rearrange("p (g n) -> p g n", n=P) for u in (u1, u2))
                dve.wait_ge(w_conv_in, 16)
                dve.tensor_tensor(v1[:, 0:FULL, :], taps(0, FULL), taps(2, FULL), ALU.add).then_inc(w_step, 1)
                dve.tensor_copy(v1[:, FULL:, :], taps(0, GROUPS)[:, FULL:, :]).then_inc(w_step, 1)
                dve.wait_ge(w_step, 2)
                dve.tensor_tensor(v2, v1, taps(1, GROUPS), ALU.subtract).then_inc(w_step, 1)
                dve.wait_ge(w_step, 3)
                dve.tensor_tensor(v1, v1, taps(1, GROUPS), ALU.add).then_inc(w_step, 1)
                dve.wait_ge(w_step, 4)

            def split_scaled(hi, lo, src, scale, k):
                dve.tensor_scalar(hi, src, scale, None, ALU.mult).then_inc(w_hi_set, 1)
                dve.wait_ge(w_hi_set, k)
                dve.scalar_tensor_tensor(out=lo, in0=src, scalar=scale, in1=hi.bitcast(F32),
                                         op0=ALU.mult, op1=ALU.subtract).then_inc(w_lo_set, 1)

            def split_u(m, u, k):
                at = slice(W_U[m], W_U[m] + GROUPS * P)
                split_scaled(w_hi[:, at], w_lo[:, at], u, 0.5, k)

            def split_g2(k):
                split_scaled(used(w_hi, 3, FULL), used(w_lo, 3, FULL), taps(2, FULL), -1.0, k)

            dve.wait_ge(se_zero, 2)
            dve.wait_ge(w_first_in, 16 * 3)
            split_weights(W_C1, W_SE + SOFF, 1)
            dve.wait_ge(x_hi_set, 1)
            dve.tensor_tensor(x_lo[0][:], x_f[0][:], x_hi[0][:].bitcast(F32), ALU.subtract).then_inc(x_lo_set, 1)
            dve.wait_ge(v_in, 16 * 3)
            dve.tensor_scalar(bn_var[:], vecs[:, V1:V2 + 1:V2 - V1], EPS, None, ALU.add).then_inc(bn_eps, 1)
            dve.wait_ge(bn_rstd, 1)
            for k, (g, b, m, sc, sh) in enumerate(((G1, B1, M1, SC1, SH1), (G2, B2, M2, SC2, SH2))):
                dve.tensor_tensor(dv[:, sc:sc + 1], vecs[:, g:g + 1], bn_var[:, k:k + 1],
                                  ALU.mult).then_inc(dv_step, 1)
                dve.wait_ge(dv_step, 2 * k + 1)
                dve.tensor_tensor(bn_var[:, k:k + 1], vecs[:, m:m + 1], dv[:, sc:sc + 1],
                                  ALU.mult).then_inc(dv_step, 1)
                dve.wait_ge(dv_step, 2 * k + 2)
                dve.tensor_tensor(dv[:, sh:sh + 1], vecs[:, b:b + 1], bn_var[:, k:k + 1], ALU.subtract)
            dve.tensor_tensor(dv[:, HB_R:HB_Z + 1], vecs[:, BI_R:BI_Z + 1], vecs[:, BH_R:BH_Z + 1],
                              ALU.add).then_inc(dv_step, 1)
            dve.wait_ge(dv_step, 5)
            dve.tensor_scalar(dv[:, HB_R:HB_Z + 1], dv[:, HB_R:HB_Z + 1], 0.5, None, ALU.mult)
            dve.tensor_scalar(dv[:, HB_N:HB_N + 1], vecs[:, BH_N:BH_N + 1], 0.5, None,
                              ALU.mult).then_inc(dv_set, 1)
            sum_taps()
            messages_and_s(0, False, False, s_only=True)
            score_rows(0)
            rest_of_messages()
            split_u(2, u2, 2)
            msg_low(0, 0)
            split_u(1, u1, 3)
            split_g2(4)
            runs(dve, batch)
            add_m0_or_m3(B - 1, 1)
            add_m0_or_m3(B - 1, 0)
            norm_measure(B - 2, (0, NC))
            n_low(B - 1)
            norm_variance(B - 2, (0, NC))
            c_even_low(B - 1)
            norm_apply(B - 2, 0)
            dve.wait_ge(xg_in, 16 * B)
            for h in range(2):
                r, z, n, x = (t[:, half[h]] for t in (g_r, z_last, g_n, x_gate))
                dve.wait_ge(r_act, B + h)
                dve.wait_ge(hn_act, B + h)
                dve.scalar_tensor_tensor(out=n, in0=r, scalar=1.0, in1=n, op0=ALU.add,
                                         op1=ALU.mult).then_inc(rn_set, 1)
                dve.wait_ge(in_ready, B + h)
                dve.wait_ge(rn_set, B + h)
                dve.tensor_tensor(r, ps_n[:, half[h]], n, ALU.add).then_inc(pre_n_set, 1)
                dve.wait_ge(z_act, B + h)
                dve.wait_ge(pre_n_set, B + h)
                dve.scalar_tensor_tensor(out=n, in0=z, scalar=3.0, in1=x, op0=ALU.add,
                                         op1=ALU.mult).then_inc(p_set, 1)
                dve.wait_ge(n_act, B + h)
                dve.wait_ge(p_set, B + h)
                dve.scalar_tensor_tensor(out=z, in0=z, scalar=-1.0, in1=r, op0=ALU.add,
                                         op1=ALU.mult).then_inc(q_set, 1)
                dve.wait_ge(q_set, B + h)
                dve.tensor_tensor(n, n, z, ALU.subtract).then_inc(y_set, 1)
            for h in range(2):
                chunks = (h * NC // 2, (h + 1) * NC // 2)
                norm_measure(B - 1 + h, chunks)
                norm_variance(B - 1 + h, chunks)
            dve.wait_ge(y_out_free, 16 + 32 * (B - 1))
            norm_apply(B, 1)

        @block.gpsimd
        def _(pool):
            pool.memset(neg_half[:], -0.5).then_inc(consts_set, 1)
            pool.memset(ident[:], 0.0).then_inc(ident_zero, 1)
            pool.wait_ge(ident_zero, 1)
            pool.affine_select(out=ident[:], in_=ident[:], compare_op=ALU.not_equal, fill=1.0, base=0,
                               pattern=[[-1, P]], channel_multiplier=1).then_inc(ident_set, 1)
            pool.wait_ge(consts_set, 1)
            pool.wait_ge(bn_eps, 1)
            pool.tensor_tensor(bn_var[:], bn_var[:], neg_half[:, 0:2], ALU.pow).then_inc(bn_rstd, 1)

            def norm_scale(n, of=slice(0, NC)):
                pool.wait_ge(var_set, n + 1)
                pool.tensor_tensor(rstd[:, of], rstd[:, of], neg_half[:, of], ALU.pow).then_inc(rstd_set, 1)
                pool.wait_ge(rstd_set, n + 1)
                pool.tensor_tensor(shift[:, of], norm_m[:, of], rstd[:, of], ALU.mult).then_inc(shift_set, 1)

            def x_low(n, p):
                pool.wait_ge(x_hi_set, n + 1)
                pool.tensor_tensor(x_lo[p][:], x_f[p][:], x_hi[p][:].bitcast(F32),
                                   ALU.subtract).then_inc(x_lo_set, 1)

            def differences(n, d):
                pool.wait_ge({2: h_f_set, 1: d_lo_set[2], 0: d_lo_set[1]}[d], n + 1)
                a, z, op = ((0, 2, ALU.subtract), (1, 2, ALU.add), (2, 1, ALU.subtract))[d]
                at = [h_f[:, k:k + 2 * DW].rearrange("p (t q) -> p q t", q=2) for k in (a, z)]
                pool.tensor_tensor(d_f[:], at[0], at[1], op).then_inc(d_f_set[d], 1)

            def d_low(n, d):
                pool.wait_ge(d_hi_set[d], n + 1)
                pool.tensor_tensor(d_lo[d][:], d_f[:], d_hi[d][:].bitcast(F32),
                                   ALU.subtract).then_inc(d_lo_set[d], 1)

            def c_odd_low(n):
                pool.wait_ge(c_hi_set, 2 * n + 1)
                pool.tensor_tensor(c_lo[:, 1::2], c_f[:], c_hi[:, 1::2].bitcast(F32),
                                   ALU.subtract).then_inc(c_lo_set[1], 1)

            def add_x(n, p):
                pool.wait_ge(m2_set, n + 1)
                x = x_f[p][:].rearrange("p (t q) -> p q t", q=2)
                pool.tensor_tensor(ab[:, 0, :], x[:, 0, :], m2_f[:], ALU.add)
                pool.tensor_tensor(ab[:, 1, :], x[:, 1, :], m2_f[:], ALU.subtract).then_inc(x_m2_set, 1)

            def blend(g):
                pool.wait_ge(q_set, g + 1)
                pool.tensor_tensor(g_n, g_n, g_z, ALU.subtract).then_inc(y_set, 1)

            def batch(b, p, first, last):
                differences(b, 1)
                d_low(b, 1)
                differences(b, 0)
                if not first and not last:
                    x_low(b + 1, 1 - p)
                d_low(b, 0)
                if first:
                    x_low(b + 1, 1 - p)
                if first:
                    pool.wait_ge(w_g0_hi_set, 1)
                    pool.tensor_tensor(used(w_lo, 0, GROUPS), taps(0, GROUPS),
                                       used(w_hi, 0, GROUPS).bitcast(F32), ALU.subtract).then_inc(w_g0_lo_set, 1)
                add_x(b, p)
                if not last:
                    differences(b + 1, 2)
                if not first:
                    blend(b - 1)
                if not last:
                    d_low(b + 1, 2)
                if first:
                    pool.wait_ge(w_gates_hi_set, 1)
                    pool.tensor_tensor(w_lo[:, W_HH:W_C2], w_f[:, W_HH:W_C2],
                                       w_hi[:, W_HH:W_C2].bitcast(F32), ALU.subtract).then_inc(w_gates_lo_set, 1)
                if not first and not last:
                    norm_scale(b - 1)
                c_odd_low(b)
                if last:
                    norm_scale(b - 1)

            pool.wait_ge(pads_set, 1)
            differences(0, 2)
            d_low(0, 2)
            runs(pool, batch)
            norm_scale(B - 1, slice(0, NC // 2))
            norm_scale(B, slice(NC // 2, NC))


_ORDER = ["xT", "adjT", "w_c1", "w_msg", "w_se", "w_hh", "w_ih", "w_c2", "vec", "b_msg", "b_se"]


def kernel(**inputs):
    import numpy as np
    import concourse.bacc as bacc
    from concourse.bass_utils import run_bass_kernel_spmd

    a = {k.replace("L0_gnn_", ""): np.asarray(v) for k, v in inputs.items()}
    d = a["x"].shape[-1]
    arrays = {
        "xT": a["x"].transpose(0, 2, 1),
        "adjT": a["adj"].transpose(0, 2, 1),
        "w_c1": a["conv1_w"][:, :, 0].T,
        "w_msg": a["w_msg"].T,
        "w_se": a["w_se"].T,
        "w_hh": a["w_hh"].T,
        "w_ih": a["w_ih"].T,
        "w_c2": a["conv2_w"].transpose(1, 2, 0).reshape(d, -1),
        "vec": np.stack([a["bn1_g"], a["bn1_b"], a["bn1_m"], a["bn1_v"],
                         a["bn2_g"], a["bn2_b"], a["bn2_m"], a["bn2_v"],
                         *a["b_ih"].reshape(3, d), *a["b_hh"].reshape(3, d)], axis=1),
        "b_msg": a["b_msg"],
        "b_se": a["b_se"],
    }
    arrays = {k: np.ascontiguousarray(v) for k, v in arrays.items()}
    nc = bacc.Bacc("TRN2", target_bir_lowering=False, num_devices=1)
    args = [nc.dram_tensor(f"{n}_in", arrays[n].shape, F32, kind="ExternalInput").ap() for n in _ORDER]
    out = nc.dram_tensor("out", a["x"].shape, F32, kind="ExternalOutput").ap()
    build(nc, *args, out)
    r = run_bass_kernel_spmd(nc, [{f"{n}_in": arrays[n] for n in _ORDER}], core_ids=[0])
    return r.results[0]["out"]
```
